# Optimizing a Trainium2 kernel written in Bass

```python
import numpy as np
import jax
import jax.numpy as jnp

def _softmax(x, axis=-1):
    return jax.nn.softmax(x, axis=axis)

def _gelu(x):
    return jax.nn.gelu(x, approximate=True)

def _silu(x):
    return jax.nn.silu(x)

def _sigmoid(x):
    return jax.nn.sigmoid(x)

def _layernorm(x, axis=-1, eps=1e-05):
    m = jnp.mean(x, axis=axis, keepdims=True)
    v = jnp.var(x, axis=axis, keepdims=True)
    return (x - m) / jnp.sqrt(v + eps)

def _scatter_add(tgt, idx, src, axis=0):
    return tgt.at[idx].add(src)

def _segment_sum(src, seg, n):
    return jax.ops.segment_sum(src, seg, n)
kernel_name = 'mk_seq_postln_d1_jaxref_r8_237d5a'

def setup_inputs(seed: int=0):
    np.random.seed(seed)
    _w = jnp.asarray

    def _L0_attn_setup():
        import jax, jax.numpy as jnp
        import numpy as np
        NEG_INF = -1e+30

        def rotary_pos_emb(x):
            B, T, H, D = x.shape
            exponents = (jnp.arange(0, D, 2)[:D // 2] // D).astype(jnp.float32)
            freqs = 1.0 / jnp.power(jnp.float32(1000.0), exponents)
            theta = jnp.arange(T, dtype=jnp.float32)[:, None] * freqs[None, :]
            cos = jnp.cos(theta)[None, :, None, :]
            sin = jnp.sin(theta)[None, :, None, :]
            xr = x.astype(jnp.float32).reshape(B, T, H, D // 2, 2)
            x0, x1 = (xr[..., 0], xr[..., 1])
            out = jnp.stack([x0 * cos - x1 * sin, x0 * sin + x1 * cos], axis=-1)
            return out.reshape(B, T, H, D).astype(x.dtype)

        def attention_fwd(x, wq, wk, wv, wo, n_heads=32):
            B, T, C = x.shape
            hd = C // n_heads
            xq = (x @ wq.T).reshape(B, T, n_heads, hd)
            xk = (x @ wk.T).reshape(B, T, n_heads, hd)
            xv = (x @ wv.T).reshape(B, T, n_heads, hd)
            xq = rotary_pos_emb(xq)
            xk = rotary_pos_emb(xk)
            scale = hd ** (-0.5)
            scores = jnp.einsum('bqhd,bkhd->bhqk', xq, xk) * scale
            causal = jnp.tril(jnp.ones((T, T), dtype=bool))
            scores = jnp.where(causal[None, None], scores, NEG_INF)
            probs = jax.nn.softmax(scores.astype(jnp.float32), axis=-1).astype(xq.dtype)
            out = jnp.einsum('bhqk,bkhd->bqhd', probs, xv).reshape(B, T, C)
            return out @ wo.T
        key = jax.random.key(seed)
        ks = jax.random.split(key, 5)
        B, T, C = (2, 256, 512)
        s = 0.02
        return {'x': jax.random.normal(ks[0], (B, T, C), jnp.float32), 'wq': jax.random.normal(ks[1], (C, C), jnp.float32) * s, 'wk': jax.random.normal(ks[2], (C, C), jnp.float32) * s, 'wv': jax.random.normal(ks[3], (C, C), jnp.float32) * s, 'wo': jax.random.normal(ks[4], (C, C), jnp.float32) * s}
    _L0_attn_in = _L0_attn_setup()

    def _L0_ffn_setup():
        import jax, jax.numpy as jnp
        import numpy as np
        RMS_EPS = 1e-05
        key = jax.random.key(seed)
        k1, k2, k3, k4 = jax.random.split(key, 4)
        B, S, H, I = (1, 256, 512, 1792)
        x = jax.random.normal(k1, (B, S, H), dtype=jnp.float32)
        ln_w = jnp.ones((H,), dtype=jnp.float32)
        gate_w = jax.random.normal(k2, (I, H), dtype=jnp.float32) * 0.02
        up_w = jax.random.normal(k3, (I, H), dtype=jnp.float32) * 0.02
        down_w = jax.random.normal(k4, (H, I), dtype=jnp.float32) * 0.02
        return {'x': x, 'ln_w': ln_w, 'gate_w': gate_w, 'up_w': up_w, 'down_w': down_w}
    _L0_ffn_in = _L0_ffn_setup()
    _d = {'L0_attn_x': _L0_attn_in['x'], 'L0_attn_wq': _L0_attn_in['wq'], 'L0_attn_wk': _L0_attn_in['wk'], 'L0_attn_wv': _L0_attn_in['wv'], 'L0_attn_wo': _L0_attn_in['wo'], 'L0_ffn_ln_w': _L0_ffn_in['ln_w'], 'L0_ffn_gate_w': _L0_ffn_in['gate_w'], 'L0_ffn_up_w': _L0_ffn_in['up_w'], 'L0_ffn_down_w': _L0_ffn_in['down_w']}
    _x0 = _d['L0_attn_x']
    _d['L0_attn_x'] = jax.random.normal(jax.random.fold_in(jax.random.key(seed), 1), (2, 1024, 512), dtype=_x0.dtype)
    del _x0
    return _d

def reference(L0_attn_x, L0_attn_wq, L0_attn_wk, L0_attn_wv, L0_attn_wo, L0_ffn_ln_w, L0_ffn_gate_w, L0_ffn_up_w, L0_ffn_down_w):

    def _L0_attn_ref(x, wq, wk, wv, wo):
        import jax, jax.numpy as jnp
        import numpy as np
        NEG_INF = -1e+30

        def rotary_pos_emb(x):
            B, T, H, D = x.shape
            exponents = (jnp.arange(0, D, 2)[:D // 2] // D).astype(jnp.float32)
            freqs = 1.0 / jnp.power(jnp.float32(1000.0), exponents)
            theta = jnp.arange(T, dtype=jnp.float32)[:, None] * freqs[None, :]
            cos = jnp.cos(theta)[None, :, None, :]
            sin = jnp.sin(theta)[None, :, None, :]
            xr = x.astype(jnp.float32).reshape(B, T, H, D // 2, 2)
            x0, x1 = (xr[..., 0], xr[..., 1])
            out = jnp.stack([x0 * cos - x1 * sin, x0 * sin + x1 * cos], axis=-1)
            return out.reshape(B, T, H, D).astype(x.dtype)

        def attention_fwd(x, wq, wk, wv, wo, n_heads=32):
            B, T, C = x.shape
            hd = C // n_heads
            xq = (x @ wq.T).reshape(B, T, n_heads, hd)
            xk = (x @ wk.T).reshape(B, T, n_heads, hd)
            xv = (x @ wv.T).reshape(B, T, n_heads, hd)
            xq = rotary_pos_emb(xq)
            xk = rotary_pos_emb(xk)
            scale = hd ** (-0.5)
            scores = jnp.einsum('bqhd,bkhd->bhqk', xq, xk) * scale
            causal = jnp.tril(jnp.ones((T, T), dtype=bool))
            scores = jnp.where(causal[None, None], scores, NEG_INF)
            probs = jax.nn.softmax(scores.astype(jnp.float32), axis=-1).astype(xq.dtype)
            out = jnp.einsum('bhqk,bkhd->bqhd', probs, xv).reshape(B, T, C)
            return out @ wo.T
        return attention_fwd(x, wq, wk, wv, wo)

    def _L0_ffn_ref(x, ln_w, gate_w, up_w, down_w):
        import jax, jax.numpy as jnp
        import numpy as np
        RMS_EPS = 1e-05
        var = jnp.mean(jnp.square(x), axis=-1, keepdims=True)
        nx = x * jax.lax.rsqrt(var + RMS_EPS) * ln_w
        g = jnp.einsum('bsh,ih->bsi', nx, gate_w)
        u = jnp.einsum('bsh,ih->bsi', nx, up_w)
        return jnp.einsum('bsi,hi->bsh', jax.nn.silu(g) * u, down_w)
    x = L0_attn_x
    x = _layernorm(x + _L0_attn_ref(x, L0_attn_wq, L0_attn_wk, L0_attn_wv, L0_attn_wo), axis=-1)
    x = _layernorm(x + _L0_ffn_ref(x, L0_ffn_ln_w, L0_ffn_gate_w, L0_ffn_up_w, L0_ffn_down_w), axis=-1)
    return x

_drawn_inputs = setup_inputs


def setup_inputs(seed=0):
    import zlib

    import numpy as np

    out = dict(_drawn_inputs(seed))
    spreads = {'L0_ffn_ln_w': (1.0, 0.2)}
    factors = {'L0_attn_wq': 8.0, 'L0_attn_wk': 8.0, 'L0_attn_wv': 3.126, 'L0_attn_wo': 3.157}
    for name, (base, spread) in spreads.items():
        noise = np.random.default_rng([zlib.crc32(name.encode()), seed]).standard_normal(out[name].shape)
        drawn = base * np.exp(spread * noise) if base else spread * noise
        out[name] = jnp.asarray(drawn.astype(out[name].dtype))
    for name, factor in factors.items():
        out[name] = (out[name] * factor).astype(out[name].dtype)
    return out
```

```python
from contextlib import ExitStack

import concourse.bass as bass
from concourse import mybir

F32 = mybir.dt.float32
F32R = mybir.dt.float32r
ALU = mybir.AluOpType
ACT = mybir.ActivationFunctionType
AX = mybir.AxisListType

P = 128
BATCH, SEQ, DIM = 2, 1024, 512
TOK = BATCH * SEQ
HEADS = 32
HD = DIM // HEADS
HALF = HD // 2
INNER = 1792
KT = DIM // P
IT = INNER // P
BLK = 512
NBLK = TOK // BLK
ST = BLK // P
QB = SEQ // P
SCALE = float(HD) ** -0.5
EPS = 1e-5
MASKED = -1e30
LEAST = -3e38

STEPS = HEADS // 2 * BATCH
SLOTS = 4
PARTS = 4 * HD
MROW = P - 2


def chunks(n):
    return [(c, min(512, n - c)) for c in range(0, n, 512)]


MAX_UNITS = [(qb, h, c, w) for qb in range(QB) for c, w in chunks((qb + 1) * P) for h in range(2)]
UNITS = len(MAX_UNITS)
ST_PAIRS = [(kb, c, max(c * BLK, kb * P), (c + 1) * BLK - max(c * BLK, kb * P))
            for kb in range(QB) for c in range(kb * P // BLK, SEQ // BLK)]
PAIRS_STEP = len(ST_PAIRS)
MAX_BANKS, ST_RING, P_RING = 3, 2, 6
assert UNITS % MAX_BANKS == 0 and PAIRS_STEP % ST_RING == 0 and PAIRS_STEP % P_RING == 0


def pairs_of(kb):
    return [p for p in range(PAIRS_STEP) if ST_PAIRS[p][0] == kb]


def at_least(engine, sem, value):
    if not isinstance(value, int) or value > 0:
        engine.wait_ge(sem, value)


def for_steps(engine, body):
    for t in range(SLOTS):
        body(t, t)
    with engine.Fori(1, STEPS // SLOTS) as i:
        for j in range(SLOTS):
            body(i * SLOTS + j, j)


class Place:

    def __init__(self, nc, start):
        self.nc, self.at = nc, start

    def __call__(self, name, shape, dt=F32):
        size = 4
        for n in shape[1:]:
            size *= n
        tensor = self.nc.alloc_sbuf_tensor_at(name, shape, dt, offset=self.at)
        self.at += (size + 31) // 32 * 32
        return tensor


def layer_kernel(nc, x, xT, wqT, wkT, wvT, woT, ln_w, gateT, upT, downT, cos, sin, out):
    ctx = ExitStack()
    with ctx:
        def sem(name):
            return ctx.enter_context(nc.semaphore(name))

        qk_dram = nc.dram_tensor("qk_parts", (2, HEADS, 2, HD, TOK), F32, kind="Internal").ap()
        o_dram = nc.dram_tensor("attn_raw", (HEADS, 2 * HD, TOK), F32, kind="Internal").ap()
        r_dram = nc.dram_tensor("sum_recip", (HEADS, TOK), F32, kind="Internal").ap()

        BASE = 16 * 1024 + 256
        fixed = Place(nc, BASE)
        ident = fixed("ident", [P, P])
        lnw_sb = fixed("lnw_sb", [P, KT])
        mhalf = fixed("mhalf", [P, ST])
        stats = fixed("stats", [P, 2, ST, 6])
        mv1 = fixed("mv1", [P, ST, 2])
        mv2 = fixed("mv2", [P, ST, 2])
        var_eps = fixed("var_eps", [P, ST])
        rstd1 = fixed("rstd1", [P, ST])
        ms_eps = fixed("ms_eps", [P, ST])
        rms = fixed("rms", [P, ST])
        var_eps2 = fixed("var_eps2", [P, ST])
        rstd2 = fixed("rstd2", [P, ST])
        sums = fixed("sums", [P, BLK])
        TOP = 224 * 1024 - 64
        v_sb = Place(nc, TOP - TOK // P * DIM * 4)("v_sb", [P, TOK // P, DIM])

        a = Place(nc, fixed.at)
        w_raw = [a(f"w_raw{n}", [P, KT, DIM]) for n in range(3)]
        x_raw = [a(f"x_raw{j}", [P, KT, BLK]) for j in range(2)]
        w_hi = [a(f"w_hi{n}", [P, KT, DIM], F32R) for n in range(3)]
        w_lo = [a(f"w_lo{n}", [P, KT, DIM], F32R) for n in range(3)]
        x_hi = [a(f"x_hi{j}", [P, KT, BLK], F32R) for j in range(2)]
        x_lo = [a(f"x_lo{j}", [P, KT, BLK], F32R) for j in range(2)]
        cos_sb = a("cos_sb", [P, SEQ])
        sin_sb = a("sin_sb", [P, SEQ])
        term = [a(f"term{n}", [P, BLK]) for n in range(4)]
        rot = [a(f"rot{r}", [P, 2, BLK]) for r in range(2)]
        rot_hi = [a(f"rot_hi{r}", [P, 2, BLK], F32R) for r in range(2)]
        rot_lo = [a(f"rot_lo{r}", [P, 2, BLK], F32R) for r in range(2)]
        assert a.at <= TOP - TOK // P * DIM * 4, a.at

        b = Place(nc, fixed.at)
        gate_sb = b("gate_sb", [P, KT, INNER])
        up_sb = b("up_sb", [P, KT, INNER])
        d = Place(nc, b.at)
        q_st = [b(f"q_st{s}", [P, 2, SEQ], F32R) for s in range(SLOTS)]
        k_st = [b(f"k_st{s}", [P, 2, SEQ], F32R) for s in range(SLOTS)]
        probs = b("probs", [P, P_RING, 2, BLK])
        v_pair = [b(f"v_pair{r}", [P, QB, 2, 2 * HD]) for r in range(2)]
        mask = b("mask", [P, BLK])
        masked = [b(f"masked{n}", [P, BLK]) for n in range(MAX_BANKS + 1)]
        row_max = b("row_max", [P, 2, 2, QB])
        m_parts = b("m_parts", [P, 2, 2, QB], F32R)
        m_turned = [b(f"m_turned{s}", [P, 32]) for s in range(SLOTS)]
        o_sb = [b(f"o_sb{r}", [P, BLK]) for r in range(2)]
        assert b.at <= TOP - TOK // P * DIM * 4, b.at

        down_sb = d("down_sb", [P, IT, DIM])
        wo_hi = d("wo_hi", [P, KT, DIM], F32R)
        wo_lo = d("wo_lo", [P, KT, DIM], F32R)
        attn = d("attn", [P, KT, BLK])
        norm_tok = attn
        recip = [d(f"recip{r}", [P, BLK]) for r in range(2)]
        attn_hi = d("attn_hi", [P, KT, BLK], F32R)
        attn_lo = d("attn_lo", [P, KT, BLK], F32R)
        wo_raw = d("res0", [P, ST, DIM])
        res = [wo_raw, d("res1", [P, ST, DIM])]
        nx_hi = d("nx_hi", [P, KT, BLK], F32R)
        nx_lo = d("nx_lo", [P, KT, BLK], F32R)
        g_hi = [d(f"g_hi{r}", [P, KT, P], F32R) for r in range(2)]
        g_lo = [d(f"g_lo{r}", [P, KT, P], F32R) for r in range(2)]
        u_hi = [d(f"u_hi{r}", [P, KT, P], F32R) for r in range(2)]
        u_lo = [d(f"u_lo{r}", [P, KT, P], F32R) for r in range(2)]
        d_hi = [d(f"d_hi{r}", [P, DIM], F32R) for r in range(2)]
        d_lo = [d(f"d_lo{r}", [P, DIM], F32R) for r in range(2)]
        silu = d("silu", [P, BLK])
        hid = d("hid", [P, BLK])
        h_hi = [d(f"h_hi{r}", [P, BLK], F32R) for r in range(2)]
        h_lo = [d(f"h_lo{r}", [P, BLK], F32R) for r in range(2)]
        assert d.at <= TOP, d.at

        psum = ctx.enter_context(nc.psum_tensor("psum", [P, 8, BLK], F32))
        bank = [psum[:, n, :] for n in range(8)]
        proj_ps = [bank[0:2], bank[2:4]]
        v_ps = bank[4:6]
        max_ps = bank[0:3]
        st_ps = [psum[:, 3 + 2 * n:5 + 2 * n, :] for n in range(ST_RING)]
        o_ps = bank[7]
        y_ps = bank[0:4]
        gate_ps, up_ps = bank[4], bank[5]
        c_ps = bank[6:8]

        tables_in = sem("tables_in")
        w_in = [sem(f"w_in{n}") for n in range(3)]
        x_in = [sem(f"x_in{j}") for j in range(2)]
        w_hi_done = sem("w_hi_done")
        w_lo_done = sem("w_lo_done")
        x_hi_done = sem("x_hi_done")
        x_lo_done = sem("x_lo_done")
        proj_done = sem("proj_done")
        proj_free = sem("proj_free")
        term_done = sem("term_done")
        rot_free = sem("rot_free")
        rot_done = sem("rot_done")
        rot_hi_done = sem("rot_hi_done")
        rot_lo_done = sem("rot_lo_done")
        qk_stored = [sem(f"qk_stored{r}") for r in range(2)]
        v_done = sem("v_done")
        v_free = sem("v_free")
        setup_done = sem("setup_done")
        stack_const = sem("stack_const")
        stack_in = [sem(f"stack_in{s}") for s in range(SLOTS)]
        max_scores = sem("max_scores")
        max_taken = sem("max_taken")
        m_step = sem("m_step")
        m_turned_done = sem("m_turned_done")
        m_in = [sem(f"m_in{s}") for s in range(SLOTS)]
        st_scores = sem("st_scores")
        clamped = sem("clamped")
        exp_done = sem("exp_done")
        v_pair_done = sem("v_pair_done")
        causal_done = sem("causal_done")
        pv_done = sem("pv_done")
        o_copied = sem("o_copied")
        o_stored = [sem(f"o_stored{r}") for r in range(2)]
        dve_waited = sem("dve_waited")
        pool_waited = sem("pool_waited")
        ffn_w_in = sem("ffn_w_in")
        down_in = sem("down_in")
        wo_in = sem("wo_in")
        wo_hi_done = sem("wo_hi_done")
        wo_lo_done = sem("wo_lo_done")
        sums_in = sem("sums_in")
        recip_done = sem("recip_done")
        recip_stored = sem("recip_stored")
        attn_in = sem("attn_in")
        recip_in = [sem(f"recip_in{r}") for r in range(2)]
        res_in = [sem(f"res_in{r}") for r in range(2)]
        attn_scaled = sem("attn_scaled")
        attn_hi_done = sem("attn_hi_done")
        attn_lo_done = sem("attn_lo_done")
        c_done = sem("c_done")
        sum1_done = sem("sum1_done")
        stats_done = sem("stats_done")
        mv1_done = sem("mv1_done")
        pool_step = sem("pool_step")
        rstd1_done = sem("rstd1_done")
        norm1_done = sem("norm1_done")
        norm_tok_done = sem("norm_tok_done")
        turned_done = sem("turned_done")
        nx_hi_done = sem("nx_hi_done")
        nx_lo_done = sem("nx_lo_done")
        gu_hi_done = sem("gu_hi_done")
        gu_lo_done = sem("gu_lo_done")
        gate_done = sem("gate_done")
        up_done = sem("up_done")
        silu_done = sem("silu_done")
        hid_done = sem("hid_done")
        h_hi_done = sem("h_hi_done")
        h_lo_done = sem("h_lo_done")
        d_hi_done = sem("d_hi_done")
        d_lo_done = sem("d_lo_done")
        down_done = sem("down_done")
        sum2_done = sem("sum2_done")
        mv2_done = sem("mv2_done")
        rstd2_done = sem("rstd2_done")
        out_ready = sem("out_ready")
        out_stored = [sem(f"out_stored{r}") for r in range(2)]

        def plain(ap):
            return ap.bitcast(F32)

        def by_tile(dram):
            return dram.rearrange("(k p) n -> p k n", p=P)

        xT_tiles, x_tiles, out_tiles = by_tile(xT), by_tile(x), by_tile(out)
        PAIRS = [(0, 0), (0, 1), (1, 0)]
        FFN_STEPS = IT

        def ffn_done(n, i):
            return n * FFN_STEPS + i + 1

        block = ctx.enter_context(nc.Block())

        @block.sync
        def _(sp):
            sp.dma_start(w_raw[0][:], by_tile(wqT)).then_inc(w_in[0], 16)
            sp.dma_start(x_raw[0][:], xT_tiles[:, :, 0:BLK]).then_inc(x_in[0], 16)
            sp.dma_start(cos_sb[:], cos.broadcast_to((P, SEQ))).then_inc(tables_in, 16)
            sp.dma_start(sin_sb[:], sin.broadcast_to((P, SEQ))).then_inc(tables_in, 16)
            sp.dma_start(w_raw[1][:], by_tile(wkT)).then_inc(w_in[1], 16)
            sp.dma_start(w_raw[2][:], by_tile(wvT)).then_inc(w_in[2], 16)
            sp.dma_start(x_raw[1][:], xT_tiles[:, :, BLK:2 * BLK]).then_inc(x_in[1], 16)
            sp.dma_start(lnw_sb[:], ln_w).then_inc(tables_in, 16)
            for tb in range(NBLK):
                if 1 <= tb < NBLK - 1:
                    sp.wait_ge(x_lo_done, KT * tb)
                    sp.dma_start(x_raw[(tb + 1) % 2][:], xT_tiles[:, :, (tb + 1) * BLK:(tb + 2) * BLK])\
                        .then_inc(x_in[(tb + 1) % 2], 16)
                for g in range(4):
                    sp.wait_ge(rot_lo_done, 4 * tb + g + 1)
                    heads = slice(g % 2 * 16, g % 2 * 16 + 16)
                    for e in range(2):
                        for part, src in enumerate((rot_hi[g % 2], rot_lo[g % 2])):
                            sp.dma_start(qk_dram[g // 2, heads, part, e * HALF:(e + 1) * HALF,
                                                 tb * BLK:(tb + 1) * BLK],
                                         plain(src[:, e, :])).then_inc(qk_stored[g % 2], 16)

            for r in range(2):
                sp.wait_ge(qk_stored[r], 1 + 16 * 4 * 2 * NBLK)

            def load(t, j):
                at_least(sp, st_scores, (t - SLOTS + 1) * PAIRS_STEP)
                if isinstance(t, int) and t < SLOTS:
                    sp.wait_ge(stack_const, 2 * (t + 1))
                s, cols = j % SLOTS, slice(j % 2 * SEQ, j % 2 * SEQ + SEQ)
                for h in range(2):
                    head = (t - j % SLOTS) + j // 2 % 2 * 2 + h if not isinstance(t, int) else t // 2 * 2 + h
                    for part in range(2):
                        src = qk_dram[0, bass.ds(head, 1), part, :, cols].broadcast_to((2, HD, SEQ))
                        sp.dma_start(plain(q_st[s][part * 2 * HD:(part + 1) * 2 * HD, h, :]), src)\
                            .then_inc(stack_in[s], 16)
                    src = qk_dram[1, bass.ds(head, 1), :, :, cols].rearrange("o a r n -> o (a r) n")
                    sp.dma_start(plain(k_st[s][0:PARTS, h, :]), src.broadcast_to((2, 2 * HD, SEQ)))\
                        .then_inc(stack_in[s], 16)

            def place_maxima(t, j):
                sp.wait_ge(m_turned_done, t + 1)
                rows = plain(q_st[j % SLOTS][MROW:MROW + 2, :, :]).rearrange(
                    "p h (g c x) -> p (h g) c x", c=4, x=32)
                for c in range(4):
                    sp.dma_start(rows[:, :, c, :], m_turned[j % SLOTS][32 * c:32 * c + 32, :])\
                        .then_inc(m_in[j % SLOTS], 16)

            load(0, 0)
            load(1, 1)
            for t in range(SLOTS):
                if t == 1:
                    sp.dma_start(gate_sb[:], by_tile(gateT)).then_inc(ffn_w_in, 16)
                    sp.dma_start(up_sb[:], by_tile(upT)).then_inc(ffn_w_in, 16)
                place_maxima(t, t)
                load(t + 2, t + 2)
            with sp.Fori(1, STEPS // SLOTS - 1) as i:
                for j in range(SLOTS):
                    place_maxima(i * SLOTS + j, j)
                    if j < 2:
                        load(i * SLOTS + j + 2, j + 2)
                    else:
                        load(i * SLOTS + SLOTS + j - 2, j - 2)
            for t in range(STEPS - SLOTS, STEPS):
                place_maxima(t, t)
                if t + 2 < STEPS:
                    load(t + 2, t + 2)

            sp.wait_ge(pv_done, STEPS * QB)
            for r in range(2):
                sp.wait_ge(o_stored[r], 16 * 2 * STEPS // 2)
            sp.dma_start(wo_raw[:], by_tile(woT)).then_inc(wo_in, 16)
            sp.dma_start(down_sb[:], by_tile(downT)).then_inc(down_in, 16)
            sp.dma_start(sums[:], o_dram[:, HD, :].rearrange("h (c n) -> h c n", n=BLK)).then_inc(sums_in, 16)
            sp.wait_ge(recip_done, 1)
            sp.dma_start(r_dram.rearrange("h (c n) -> (h c) n", n=BLK), sums[:]).then_inc(recip_stored, 16)

            def load_c(n):
                cols = slice(n * BLK, (n + 1) * BLK)
                if n == 0:
                    sp.wait_ge(wo_lo_done, 1)
                if n >= 1:
                    sp.wait_ge(turned_done, n * KT)
                if n >= 2:
                    sp.wait_ge(out_stored[n % 2], 16 * (n // 2))
                sp.dma_start(res[n % 2][:], x_tiles[:, n * ST:(n + 1) * ST, :]).then_inc(res_in[n % 2], 16)
                for k in range(KT):
                    sp.dma_start(attn[:, k, :], o_dram[8 * k:8 * k + 8, 0:HD, cols]).then_inc(attn_in, 16)
                if n == 0:
                    sp.wait_ge(recip_stored, 16)
                for k in range(KT):
                    use = n * KT + k
                    at_least(sp, attn_scaled, use - 1)
                    src = r_dram[8 * k:8 * k + 8, cols].rearrange("h (o n) -> h o n", o=1)
                    sp.dma_start(recip[k % 2][:], src.broadcast_to((8, HD, BLK))).then_inc(recip_in[k % 2], 16)

            def store(n):
                sp.wait_ge(out_ready, ST * (n + 1))
                sp.dma_start(out_tiles[:, n * ST:(n + 1) * ST, :], res[n % 2][:]).then_inc(out_stored[n % 2], 16)

            load_c(0)
            for n in range(NBLK):
                if n >= 1:
                    store(n - 1)
                if n + 1 < NBLK:
                    load_c(n + 1)
            store(NBLK - 1)
            for r in range(2):
                sp.wait_ge(out_stored[r], 16 * NBLK // 2)

        @block.gpsimd
        def _(pool):
            pool.sem_inc(proj_free, 2)
            pool.sem_inc(rot_free, 2)
            pool.sem_inc(v_free, 2)
            pool.sem_inc(qk_stored[0], 1)
            pool.sem_inc(qk_stored[1], 1)
            pool.sem_inc(down_done, 1)
            nc.gpsimd.memset(mhalf[:], -0.5)
            nc.gpsimd.memset(ident[:], 0.0).then_inc(setup_done, 1)
            pool.wait_ge(setup_done, 1)
            nc.gpsimd.affine_select(out=ident[:], in_=ident[:], compare_op=ALU.not_equal, fill=1.0, base=0,
                                    pattern=[[-1, P]], channel_multiplier=1).then_inc(setup_done, 1)

            with pool.Fori(0, NBLK // 2) as n:
                for j in range(2):
                    for g in range(4):
                        use = n * 8 + j * 4 + g
                        pool.wait_ge(rot_hi_done, use + 1)
                        nc.gpsimd.tensor_tensor(rot_lo[g % 2][:], rot[g % 2][:], plain(rot_hi[g % 2][:]),
                                                ALU.subtract).then_inc(rot_lo_done, 1)
                        pool.wait_ge(rot_lo_done, use + 1)
                        pool.sem_inc(rot_free, 1)

            for r in range(2):
                pool.wait_ge(qk_stored[r], 1 + 16 * 4 * 2 * NBLK)
            pool.wait_ge(v_free, 2 + NBLK * ST)
            for s in range(SLOTS):
                nc.gpsimd.memset(plain(q_st[s][PARTS:P, :, :]), 0.0).then_inc(stack_const, 1)
                nc.gpsimd.memset(plain(k_st[s][PARTS:P, :, :]), 1.0).then_inc(stack_const, 1)
            pool.wait_ge(stack_const, 2 * SLOTS)
            for r in range(2):
                nc.gpsimd.memset(v_pair[r][:], 1.0).then_inc(setup_done, 1)
            nc.gpsimd.memset(mask[:], 0.0).then_inc(setup_done, 1)
            pool.wait_ge(setup_done, 5)
            nc.gpsimd.affine_select(out=mask[:, BLK - P:BLK], in_=mask[:, BLK - P:BLK], compare_op=ALU.is_ge,
                                    fill=MASKED, base=0, pattern=[[-1, P]], channel_multiplier=1)\
                .then_inc(setup_done, 1)

            def step(t, j):
                at_least(pool, pv_done, (t - 1) * QB)
                cols = t // 2 * 2 * HD if isinstance(t, int) else (t - j) * HD + j // 2 * 2 * HD
                src = v_sb[:, j % 2 * QB:(j % 2 + 1) * QB, bass.ds(cols, 2 * HD)]
                nc.gpsimd.tensor_copy(v_pair[j % 2][:, :, :, 0:HD],
                                      src.rearrange("p k (h d) -> p k h d", h=2)).then_inc(v_pair_done, 1)
                for kb in range(QB):
                    p = pairs_of(kb)[0]
                    pool.wait_ge(exp_done, t * PAIRS_STEP + p + 1)
                    pool.sem_inc(pool_waited, 1)
                    p2 = probs[:, p % P_RING, :, 0:P]
                    nc.gpsimd.affine_select(out=p2, in_=p2, compare_op=ALU.is_ge, fill=0.0, base=0,
                                            pattern=[[0, 2], [1, P]], channel_multiplier=-1)\
                        .then_inc(causal_done, 1)

            for_steps(pool, step)

            steps = [0]

            def link(ins):
                steps[0] += 1
                ins.then_inc(pool_step, 1)
                pool.wait_ge(pool_step, steps[0])

            def first_norm(n):
                pool.wait_ge(mv1_done, ST * (n + 1))
                if n:
                    pool.wait_ge(norm_tok_done, ST * n)
                mean_var = mv1[:, :, 1]
                link(nc.gpsimd.tensor_scalar(var_eps[:], mean_var, EPS, None, ALU.add))
                link(nc.gpsimd.tensor_tensor(rstd1[:], var_eps[:], mhalf[:], ALU.pow))
                link(nc.gpsimd.tensor_tensor(ms_eps[:], rstd1[:], rstd1[:], ALU.mult))
                link(nc.gpsimd.tensor_tensor(ms_eps[:], ms_eps[:], mean_var, ALU.mult))
                link(nc.gpsimd.tensor_scalar(ms_eps[:], ms_eps[:], EPS, None, ALU.add))
                nc.gpsimd.tensor_tensor(rms[:], ms_eps[:], mhalf[:], ALU.pow).then_inc(rstd1_done, 1)

            def second_norm(n):
                pool.wait_ge(mv2_done, ST * (n + 1))
                if n:
                    pool.wait_ge(out_ready, ST * n)
                link(nc.gpsimd.tensor_scalar(var_eps2[:], mv2[:, :, 1], EPS, None, ALU.add))
                nc.gpsimd.tensor_tensor(rstd2[:], var_eps2[:], mhalf[:], ALU.pow).then_inc(rstd2_done, 1)

            first_norm(0)
            for n in range(NBLK):
                if n >= 1:
                    second_norm(n - 1)
                if n + 1 < NBLK:
                    first_norm(n + 1)
            second_norm(NBLK - 1)

        @block.scalar
        def _(act):
            def weight_hi(n):
                act.wait_ge(w_in[n], 16)
                nc.scalar.copy(w_hi[n][:], w_raw[n][:]).then_inc(w_hi_done, 1)

            for n in range(3):
                weight_hi(n)
            with act.Fori(0, NBLK // 2) as n:
                for j in range(2):
                    act.wait_ge(x_in[j], n * 16 + 16)
                    for k in range(KT):
                        nc.scalar.copy(x_hi[j][:, k, :], x_raw[j][:, k, :]).then_inc(x_hi_done, 1)
                    for g in range(4):
                        act.wait_ge(rot_done, n * 8 + j * 4 + g + 1)
                        act.wait_ge(qk_stored[g % 2], n * 256 + j * 128 + g // 2 * 64 + 1)
                        nc.scalar.copy(rot_hi[g % 2][:], rot[g % 2][:]).then_inc(rot_hi_done, 1)
                    for s in range(ST):
                        act.wait_ge(v_done, n * 8 + j * 4 + s + 1)
                        nc.scalar.copy(v_sb[:, bass.ds(n * 8 + j * 4 + s, 1), :].rearrange("p o n -> p (o n)"),
                                       v_ps[s % 2]).then_inc(v_free, 1)

            def exps(t, kb):
                for p in pairs_of(kb):
                    _, c, q0, w = ST_PAIRS[p]
                    scores, to = st_ps[p % ST_RING], probs[:, p % P_RING]
                    act.wait_ge(st_scores, t * PAIRS_STEP + p + 1)
                    skip = P if w == P else 0
                    diagonal = q0 == kb * P
                    if diagonal:
                        square = scores[:, :, skip:skip + P]
                        nc.scalar.activation(square, square, ACT.Relu, scale=-1.0).then_inc(clamped, 1)
                    before = ST_PAIRS[(p - P_RING) % PAIRS_STEP][0]
                    at_least(act, pv_done, (t if p >= P_RING else t - 1) * QB + before + 1)
                    if diagonal:
                        if w > P:
                            nc.scalar.activation(to[:, :, P:w], scores[:, :, P:w], ACT.Exp, scale=SCALE)
                        act.wait_ge(clamped, t * QB + kb + 1)
                        nc.scalar.activation(to[:, :, 0:P], square, ACT.Exp, scale=-SCALE).then_inc(exp_done, 1)
                    else:
                        nc.scalar.activation(to, scores, ACT.Exp, scale=SCALE).then_inc(exp_done, 1)

            def output(t, j):
                act.wait_ge(pv_done, t * QB)
                r = (j - 1) % 2
                if isinstance(t, int):
                    at_least(act, o_stored[r], (t - 1) // 2 * 32)
                else:
                    act.wait_ge(o_stored[r], (t - j) * 16 + (j - 1) // 2 * 32)
                nc.scalar.copy(o_sb[r][:], o_ps).then_inc(o_copied, 1)
                act.wait_ge(o_copied, t)
                if isinstance(t, int):
                    head = (t - 1) // 2 * 2
                else:
                    head = (t - j) + (j - 1) // 2 * 2
                for c in range(2):
                    first = (j - 1) % 2 * SEQ + c * BLK
                    act.dma_start(o_dram[bass.ds(head, 2), :, first:first + BLK],
                                  o_sb[r][c * 64:(c + 1) * 64, :]).then_inc(o_stored[r], 16)

            def step(t, j):
                exps(t, 0)
                if not (isinstance(t, int) and t == 0):
                    output(t, j)
                for kb in range(1, QB):
                    exps(t, kb)

            for_steps(act, step)
            output(STEPS, STEPS)

            act.wait_ge(wo_in, 16)
            nc.scalar.copy(wo_hi[:], wo_raw[:]).then_inc(wo_hi_done, 1)

            def attn_parts(n):
                at_least(act, c_done, n * ST)
                for k in range(KT):
                    act.wait_ge(attn_scaled, n * KT + k + 1)
                    nc.scalar.copy(attn_hi[:, k, :], attn[:, k, :]).then_inc(attn_hi_done, 1)

            def turned_parts(n):
                at_least(act, up_done, n * FFN_STEPS)
                for k in range(KT):
                    act.wait_ge(turned_done, n * KT + k + 1)
                    nc.scalar.activation(nx_hi[:, k, :], c_ps[k % 2], ACT.Copy,
                                         scale=lnw_sb[:, k:k + 1]).then_inc(nx_hi_done, 1)

            def gate_up_hi(n, i, r):
                at_least(act, up_done, n * FFN_STEPS + i - 1)
                cols = slice(i * P, (i + 1) * P) if isinstance(i, int) else bass.ds(i * P, P)
                nc.scalar.copy(g_hi[r][:], gate_sb[:, :, cols]).then_inc(gu_hi_done, 1)
                nc.scalar.copy(u_hi[r][:], up_sb[:, :, cols]).then_inc(gu_hi_done, 1)

            def silu_of(n, i, r):
                act.wait_ge(gate_done, n * FFN_STEPS + i + 1)
                at_least(act, hid_done, n * FFN_STEPS + i)
                nc.scalar.activation(silu[:], gate_ps, ACT.Silu).then_inc(silu_done, 1)
                at_least(act, down_done, n * FFN_STEPS + i)
                row = i if isinstance(i, int) else None
                src = down_sb[:, row, :] if row is not None else \
                    down_sb[:, bass.ds(i, 1), :].rearrange("p o n -> p (o n)")
                nc.scalar.copy(d_hi[r][:], src).then_inc(d_hi_done, 1)

            attn_parts(0)
            act.wait_ge(ffn_w_in, 32)
            act.wait_ge(down_in, 16)
            for n in range(NBLK):
                gate_up_hi(n, 0, 0)
                turned_parts(n)
                gate_up_hi(n, 1, 1)
                silu_of(n, 0, 0)
                if n + 1 < NBLK:
                    attn_parts(n + 1)
                for first, last in ((2, 8), (8, 10), (10, IT)):
                    with act.Fori(first // 2, last // 2) as i:
                        for r in range(2):
                            gate_up_hi(n, i * 2 + r, r)
                            silu_of(n, i * 2 + (r - 1), 1 - r)
                silu_of(n, IT - 1, 1)

        @block.vector
        def _(dve):
            for n in range(3):
                dve.wait_ge(w_hi_done, n + 1)
                nc.vector.tensor_tensor(w_lo[n][:], w_raw[n][:], plain(w_hi[n][:]), ALU.subtract)\
                    .then_inc(w_lo_done, 1)
            dve.wait_ge(tables_in, 48)
            with dve.Fori(0, NBLK // 2) as n:
                for j in range(2):
                    for k in range(KT):
                        dve.wait_ge(x_hi_done, n * 8 + j * 4 + k + 1)
                        nc.vector.tensor_tensor(x_lo[j][:, k, :], x_raw[j][:, k, :], plain(x_hi[j][:, k, :]),
                                                ALU.subtract).then_inc(x_lo_done, 1)
                    cos_j, sin_j = (t[:, j * BLK:(j + 1) * BLK] for t in (cos_sb, sin_sb))
                    for g in range(4):
                        use = n * 8 + j * 4 + g
                        even, odd = proj_ps[g % 2]
                        dve.wait_ge(proj_done, use + 1)
                        nc.vector.tensor_tensor(term[0][:], even, cos_j, ALU.mult)
                        nc.vector.tensor_tensor(term[1][:], odd, sin_j, ALU.mult)
                        nc.vector.tensor_tensor(term[2][:], even, sin_j, ALU.mult)
                        nc.vector.tensor_tensor(term[3][:], odd, cos_j, ALU.mult).then_inc(term_done, 1)
                        dve.wait_ge(term_done, use + 1)
                        dve.sem_inc(proj_free, 1)
                        dve.wait_ge(rot_free, use + 1)
                        nc.vector.tensor_tensor(rot[g % 2][:, 0, :], term[0][:], term[1][:], ALU.subtract)
                        nc.vector.tensor_tensor(rot[g % 2][:, 1, :], term[2][:], term[3][:], ALU.add)\
                            .then_inc(rot_done, 1)
                        dve.wait_ge(rot_done, use + 1)

            dve.wait_ge(setup_done, 6)

            def step(t, j):
                for u, (qb, h, c, w) in enumerate(MAX_UNITS):
                    diagonal = c + w == (qb + 1) * P
                    if not diagonal:
                        dve.wait_ge(max_scores, t * UNITS + u + 1)
                    elif h == 0:
                        dve.wait_ge(max_scores, t * UNITS + u + 2)
                        dve.sem_inc(dve_waited, 1)
                    scores = max_ps[u % MAX_BANKS][:, 0:w]
                    to = row_max[:, c // BLK, h, qb:qb + 1]
                    if diagonal:
                        nc.vector.tensor_tensor_reduce(masked[u % (MAX_BANKS + 1)][:, 0:w], scores, mask[:, BLK - w:BLK], 1.0, LEAST,
                                                       ALU.add, ALU.max, to).then_inc(max_taken, 1)
                    else:
                        nc.vector.tensor_reduce(to, scores, AX.X, ALU.max).then_inc(max_taken, 1)
                dve.wait_ge(max_taken, (t + 1) * UNITS)
                late = row_max[:, 0, :, QB // 2:QB]
                nc.vector.tensor_tensor(late, late, row_max[:, 1, :, QB // 2:QB], ALU.max).then_inc(m_step, 1)
                dve.wait_ge(m_step, t * 3 + 1)
                at_least(dve, m_turned_done, t)
                nc.vector.tensor_scalar(m_parts[:, 0], row_max[:, 0], -1.0, None, ALU.mult).then_inc(m_step, 1)
                dve.wait_ge(m_step, t * 3 + 2)
                nc.vector.scalar_tensor_tensor(m_parts[:, 1], row_max[:, 0], -1.0, plain(m_parts[:, 0]),
                                               ALU.mult, ALU.subtract).then_inc(m_step, 1)
                dve.wait_ge(m_step, t * 3 + 3)
                if isinstance(t, int):
                    at_least(dve, m_in[j % SLOTS], t // SLOTS * 64)
                else:
                    dve.wait_ge(m_in[j % SLOTS], (t - j) * 16)
                nc.vector.transpose(m_turned[j % SLOTS][:], plain(m_parts[:].rearrange("p a h q -> p (a h q)")))\
                    .then_inc(m_turned_done, 1)

            for_steps(dve, step)

            dve.wait_ge(wo_hi_done, 1)
            nc.vector.tensor_tensor(wo_lo[:], wo_raw[:], plain(wo_hi[:]), ALU.subtract).then_inc(wo_lo_done, 1)
            dve.wait_ge(sums_in, 16)
            nc.vector.reciprocal(sums[:], sums[:]).then_inc(recip_done, 1)

            def attn_parts(n):
                dve.wait_ge(attn_in, 16 * KT * (n + 1))
                for k in range(KT):
                    dve.wait_ge(recip_in[k % 2], 16 * (n * KT // 2 + k // 2 + 1))
                    nc.vector.tensor_tensor(attn[:, k, :], attn[:, k, :], recip[k % 2][:], ALU.mult)\
                        .then_inc(attn_scaled, 1)
                for k in range(KT):
                    dve.wait_ge(attn_hi_done, n * KT + k + 1)
                    nc.vector.tensor_tensor(attn_lo[:, k, :], attn[:, k, :], plain(attn_hi[:, k, :]),
                                            ALU.subtract).then_inc(attn_lo_done, 1)

            def tile_stats(src, parts, to, done):
                nc.vector.bn_stats(parts, src).then_inc(stats_done, 1)
                seen[0] += 1
                dve.wait_ge(stats_done, seen[0])
                nc.vector.bn_aggr(to, parts).then_inc(done, 1)

            seen = [0]

            def first_sum(n):
                dve.wait_ge(res_in[n % 2], 16 * (n // 2 + 1))
                if n:
                    dve.wait_ge(rstd1_done, n)
                    dve.wait_ge(norm1_done, ST * n)
                for s in range(ST):
                    z = res[n % 2][:, s, :]
                    dve.wait_ge(c_done, n * ST + s + 1)
                    nc.vector.tensor_tensor(z, c_ps[s % 2], z, ALU.add).then_inc(sum1_done, 1)
                    dve.wait_ge(sum1_done, n * ST + s + 1)
                    tile_stats(z, stats[:, 0, s, :], mv1[:, s, :], mv1_done)

            def first_norm(n):
                dve.wait_ge(rstd1_done, n + 1)
                for s in range(ST):
                    z = res[n % 2][:, s, :]
                    nc.vector.tensor_scalar(z, z, mv1[:, s, 0:1], rstd1[:, s:s + 1], ALU.subtract, ALU.mult)\
                        .then_inc(norm1_done, 1)
                dve.wait_ge(attn_lo_done, KT * (n + 1))
                for s in range(ST):
                    dve.wait_ge(norm1_done, n * ST + s + 1)
                    nc.vector.tensor_scalar(norm_tok[:, s, :], res[n % 2][:, s, :], rms[:, s:s + 1], None,
                                            ALU.mult).then_inc(norm_tok_done, 1)

            def turned_parts(n):
                for k in range(KT):
                    dve.wait_ge(nx_hi_done, n * KT + k + 1)
                    nc.vector.scalar_tensor_tensor(nx_lo[:, k, :], c_ps[k % 2], lnw_sb[:, k:k + 1],
                                                   plain(nx_hi[:, k, :]), ALU.mult, ALU.subtract)\
                        .then_inc(nx_lo_done, 1)

            def gate_up_lo(n, i, r):
                done = (n * FFN_STEPS + i) * 2
                cols = slice(i * P, (i + 1) * P) if isinstance(i, int) else bass.ds(i * P, P)
                dve.wait_ge(gu_hi_done, done + 1)
                nc.vector.tensor_tensor(g_lo[r][:], gate_sb[:, :, cols], plain(g_hi[r][:]), ALU.subtract)\
                    .then_inc(gu_lo_done, 1)
                dve.wait_ge(gu_hi_done, done + 2)
                nc.vector.tensor_tensor(u_lo[r][:], up_sb[:, :, cols], plain(u_hi[r][:]), ALU.subtract)\
                    .then_inc(gu_lo_done, 1)

            def hidden(n, i, r):
                done = n * FFN_STEPS + i
                dve.wait_ge(silu_done, done + 1)
                dve.wait_ge(up_done, done + 1)
                at_least(dve, h_lo_done, done)
                nc.vector.tensor_tensor(hid[:], up_ps, silu[:], ALU.mult).then_inc(hid_done, 1)
                dve.wait_ge(hid_done, done + 1)
                at_least(dve, down_done, done)
                nc.vector.tensor_copy(h_hi[r][:], hid[:]).then_inc(h_hi_done, 1)
                dve.wait_ge(h_hi_done, done + 1)
                nc.vector.tensor_tensor(h_lo[r][:], hid[:], plain(h_hi[r][:]), ALU.subtract)\
                    .then_inc(h_lo_done, 1)
                dve.wait_ge(d_hi_done, done + 1)
                src = down_sb[:, i, :] if isinstance(i, int) else \
                    down_sb[:, bass.ds(i, 1), :].rearrange("p o n -> p (o n)")
                nc.vector.tensor_tensor(d_lo[r][:], src, plain(d_hi[r][:]), ALU.subtract).then_inc(d_lo_done, 1)

            def second_sum(n):
                dve.wait_ge(down_done, 1 + ffn_done(n, IT - 1))
                if n:
                    dve.wait_ge(rstd2_done, n)
                    dve.wait_ge(out_ready, ST * n)
                for s in range(ST):
                    z = res[n % 2][:, s, :]
                    nc.vector.tensor_tensor(z, y_ps[s], z, ALU.add).then_inc(sum2_done, 1)
                    dve.wait_ge(sum2_done, n * ST + s + 1)
                    tile_stats(z, stats[:, 1, s, :], mv2[:, s, :], mv2_done)

            def second_norm(n):
                dve.wait_ge(rstd2_done, n + 1)
                for s in range(ST):
                    z = res[n % 2][:, s, :]
                    nc.vector.tensor_scalar(z, z, mv2[:, s, 0:1], rstd2[:, s:s + 1], ALU.subtract, ALU.mult)\
                        .then_inc(out_ready, 1)

            def pairs(n, first, last):
                with dve.Fori(first // 2, last // 2) as i:
                    for r in range(2):
                        gate_up_lo(n, i * 2 + r, r)
                        hidden(n, i * 2 + (r - 1), 1 - r)

            attn_parts(0)
            first_sum(0)
            first_norm(0)
            dve.wait_ge(ffn_w_in, 32)
            dve.wait_ge(down_in, 16)
            for n in range(NBLK):
                gate_up_lo(n, 0, 0)
                turned_parts(n)
                if n:
                    second_sum(n - 1)
                gate_up_lo(n, 1, 1)
                hidden(n, 0, 0)
                if n:
                    second_norm(n - 1)
                if n + 1 < NBLK:
                    attn_parts(n + 1)
                pairs(n, 2, 8)
                if n + 1 < NBLK:
                    gate_up_lo(n, 8, 0)
                    hidden(n, 7, 1)
                    first_sum(n + 1)
                    gate_up_lo(n, 9, 1)
                    hidden(n, 8, 0)
                    first_norm(n + 1)
                else:
                    pairs(n, 8, 10)
                pairs(n, 10, IT)
                hidden(n, IT - 1, 1)
            second_sum(NBLK - 1)
            second_norm(NBLK - 1)

        @block.tensor
        def _(pe):
            def product(to, left, right, first=True, last=True):
                for n, (a_, b_) in enumerate(PAIRS):
                    mm = nc.tensor.matmul(to, left[a_], right[b_], start=first and n == 0,
                                          stop=last and n == len(PAIRS) - 1)
                return mm

            with pe.Fori(0, NBLK // 2) as n:
                for j in range(2):
                    for g in range(4):
                        use = n * 8 + j * 4 + g
                        w = g // 2
                        pe.wait_ge(w_lo_done, w + 1)
                        pe.wait_ge(proj_free, use + 1)
                        for half in range(2):
                            cols = slice((g % 2 * 2 + half) * P, (g % 2 * 2 + half + 1) * P)
                            for k in range(KT):
                                if g == 0 and half == 0:
                                    pe.wait_ge(x_lo_done, n * 8 + j * 4 + k + 1)
                                mm = product(proj_ps[g % 2][half],
                                             (w_hi[w][:, k, cols], w_lo[w][:, k, cols]),
                                             (x_hi[j][:, k, :], x_lo[j][:, k, :]), k == 0, k == KT - 1)
                        mm.then_inc(proj_done, 1)
                    for s in range(ST):
                        pe.wait_ge(w_lo_done, 3)
                        pe.wait_ge(v_free, n * 8 + j * 4 + s + 1)
                        rows = slice(s * P, (s + 1) * P)
                        for k in range(KT):
                            mm = product(v_ps[s % 2], (x_hi[j][:, k, rows], x_lo[j][:, k, rows]),
                                         (w_hi[2][:, k, :], w_lo[2][:, k, :]), k == 0, k == KT - 1)
                        mm.then_inc(v_done, 1)

            pe.wait_ge(rot_done, 4 * NBLK)
            pe.wait_ge(v_free, 2 + NBLK * ST)

            def max_scores_of(t, j, qb):
                s = j % SLOTS
                for u, (block_, h, c, w) in enumerate(MAX_UNITS):
                    if block_ != qb:
                        continue
                    at_least(pe, max_taken, t * UNITS + u + 1 - MAX_BANKS)
                    wide = max(w, 2 * P)
                    nc.tensor.matmul(max_ps[u % MAX_BANKS][:, 0:wide],
                                     q_st[s][0:MROW, h, qb * P:(qb + 1) * P],
                                     k_st[s][0:MROW, h, c:c + wide], start=True, stop=True)\
                        .then_inc(max_scores, 1)

            def st_scores_of(t, j, kb):
                s = j % SLOTS
                for p in pairs_of(kb):
                    _, c, q0, w = ST_PAIRS[p]
                    at_least(pe, exp_done, t * PAIRS_STEP + p + 1 - ST_RING)
                    wide = max(w, 2 * P)
                    q0 -= wide - w
                    for h in range(2):
                        mm = nc.tensor.matmul(st_ps[p % ST_RING][:, h, 0:wide],
                                              k_st[s][:, h, kb * P:(kb + 1) * P],
                                              q_st[s][:, h, q0:q0 + wide], start=True, stop=True)
                    mm.then_inc(st_scores, 1)

            def values(t, j, kb):
                pe.wait_ge(exp_done, t * PAIRS_STEP + pairs_of(kb)[-1] + 1)
                pe.wait_ge(causal_done, t * QB + kb + 1)
                if kb == 0:
                    pe.wait_ge(v_pair_done, t + 1)
                    at_least(pe, o_copied, t)
                for p in pairs_of(kb):
                    _, c, q0, w = ST_PAIRS[p]
                    for h in range(2):
                        rows = (c * 2 + h) * 32
                        mm = nc.tensor.matmul(o_ps[rows:rows + 2 * HD, q0 - c * BLK:q0 - c * BLK + w],
                                              v_pair[j % 2][:, kb, h, :], probs[:, p % P_RING, h, 0:w],
                                              start=kb == 0, stop=kb == (c + 1) * BLK // P - 1)
                mm.then_inc(pv_done, 1)

            def step(t, j, maxima=True, late=True, last=True):
                fixed_t = isinstance(t, int)
                if maxima:
                    s = j % SLOTS
                    pe.wait_ge(stack_in[s], t // SLOTS * 96 + 96 if fixed_t else (t - j) * 24 + 96)
                s2 = (j - 2) % SLOTS
                if late:
                    uses = (t - 2) // SLOTS * 64 + 64 if fixed_t else (t - j) * 16 + (j - 2) // SLOTS * 64 + 64
                    pe.wait_ge(m_in[s2], uses)
                for b_ in range(QB):
                    if late:
                        st_scores_of(t - 2, s2, b_)
                    if maxima:
                        max_scores_of(t, j, b_)
                    if b_ == 0:
                        if not fixed_t or t >= 3:
                            values(t - 3, (j - 3) % SLOTS, QB - 1)
                    elif late:
                        values(t - 2, s2, b_ - 1)

            for t in range(SLOTS):
                step(t, t, late=t >= 2)
            with pe.Fori(1, STEPS // SLOTS) as i:
                for j in range(SLOTS):
                    step(i * SLOTS + j, j)
            for t in range(STEPS, STEPS + 2):
                step(t, t, maxima=False)
            values(STEPS - 1, (STEPS - 1) % SLOTS, QB - 1)

            pe.wait_ge(o_copied, STEPS)
            pe.wait_ge(wo_lo_done, 1)

            def project(n):
                for s in range(ST):
                    rows = slice(s * P, (s + 1) * P)
                    at_least(pe, sum1_done, n * ST + s - 1)
                    for k in range(KT):
                        if s == 0:
                            pe.wait_ge(attn_lo_done, n * KT + k + 1)
                        mm = product(c_ps[s % 2], (attn_hi[:, k, rows], attn_lo[:, k, rows]),
                                     (wo_hi[:, k, :], wo_lo[:, k, :]), k == 0, k == KT - 1)
                    mm.then_inc(c_done, 1)

            def turn(n):
                pe.wait_ge(setup_done, 2)
                for k in range(KT):
                    if k >= 2:
                        pe.wait_ge(nx_lo_done, n * KT + k - 1)
                    for s in range(ST):
                        if k == 0:
                            pe.wait_ge(norm_tok_done, n * ST + s + 1)
                        mm = nc.tensor.transpose(c_ps[k % 2][:, s * P:(s + 1) * P],
                                                 norm_tok[:, s, k * P:(k + 1) * P], ident[:])
                    mm.then_inc(turned_done, 1)

            def gate_up(n, i, r):
                done = n * FFN_STEPS + i
                for which, (hi, lo, to, ready, used) in enumerate((
                        (g_hi[r], g_lo[r], gate_ps, gate_done, silu_done),
                        (u_hi[r], u_lo[r], up_ps, up_done, hid_done))):
                    pe.wait_ge(gu_lo_done, done * 2 + which + 1)
                    at_least(pe, used, done)
                    for k in range(KT):
                        if isinstance(i, int) and i == 0 and which == 0:
                            pe.wait_ge(nx_lo_done, n * KT + k + 1)
                        mm = product(to, (hi[:, k, :], lo[:, k, :]), (nx_hi[:, k, :], nx_lo[:, k, :]),
                                     k == 0, k == KT - 1)
                    mm.then_inc(ready, 1)

            def down(n, i, r, first=False, last=False):
                done = n * FFN_STEPS + i
                pe.wait_ge(h_lo_done, done + 1)
                pe.wait_ge(d_lo_done, done + 1)
                if first:
                    at_least(pe, sum2_done, n * ST)
                for s in range(ST):
                    rows = slice(s * P, (s + 1) * P)
                    mm = product(y_ps[s], (h_hi[r][:, rows], h_lo[r][:, rows]), (d_hi[r][:], d_lo[r][:]),
                                 first, last)
                mm.then_inc(down_done, 1)

            project(0)
            for n in range(NBLK):
                turn(n)
                gate_up(n, 0, 0)
                gate_up(n, 1, 1)
                down(n, 0, 0, first=True)
                for first, last in ((2, 8), (8, IT)):
                    with pe.Fori(first // 2, last // 2) as i:
                        for r in range(2):
                            gate_up(n, i * 2 + r, r)
                            down(n, i * 2 + (r - 1), 1 - r)
                    if first == 2 and n + 1 < NBLK:
                        project(n + 1)
                down(n, IT - 1, 1, last=True)


def kernel(L0_attn_x, L0_attn_wq, L0_attn_wk, L0_attn_wv, L0_attn_wo, L0_ffn_ln_w, L0_ffn_gate_w,
           L0_ffn_up_w, L0_ffn_down_w):
    import numpy as np
    import concourse.bacc as bacc
    from concourse.bass_utils import run_bass_kernel_spmd

    def turned(w):
        return np.ascontiguousarray(np.asarray(w).T)

    def rotary_rows(w):
        w = np.asarray(w).reshape(2, HEADS // 2, HALF, 2, DIM)
        return turned(w.transpose(0, 3, 1, 2, 4).reshape(DIM, DIM))

    position = np.arange(SEQ, dtype=np.float64)
    x = np.ascontiguousarray(np.asarray(L0_attn_x).reshape(TOK, DIM))
    arrays = {
        "x": x,
        "xT": turned(x),
        "wqT": rotary_rows(L0_attn_wq),
        "wkT": rotary_rows(L0_attn_wk),
        "wvT": turned(L0_attn_wv),
        "woT": turned(L0_attn_wo),
        "ln_w": turned(np.asarray(L0_ffn_ln_w).reshape(KT, P)),
        "gateT": turned(L0_ffn_gate_w),
        "upT": turned(L0_ffn_up_w),
        "downT": turned(L0_ffn_down_w),
        "cos": np.cos(position).astype(np.float32).reshape(1, SEQ),
        "sin": np.sin(position).astype(np.float32).reshape(1, SEQ),
    }
    nc = bacc.Bacc("TRN2", target_bir_lowering=False, num_devices=1)
    args = {name: nc.dram_tensor(name, a.shape, mybir.dt.from_np(a.dtype), kind="ExternalInput").ap()
            for name, a in arrays.items()}
    out = nc.dram_tensor("out", (TOK, DIM), F32, kind="ExternalOutput").ap()
    layer_kernel(nc, **args, out=out)
    result = run_bass_kernel_spmd(nc, [arrays], core_ids=[0])
    return result.results[0]["out"].reshape(BATCH, SEQ, DIM)
```

```python
from contextlib import ExitStack

import concourse.bass as bass
from concourse import mybir

F32 = mybir.dt.float32
F32R = mybir.dt.float32r
ALU = mybir.AluOpType
ACT = mybir.ActivationFunctionType
AX = mybir.AxisListType

P = 128
BATCH, SEQ, DIM = 2, 1024, 512
TOK = BATCH * SEQ
HEADS = 32
HD = DIM // HEADS
HALF = HD // 2
INNER = 1792
KT = DIM // P
IT = INNER // P
BLK = 512
NBLK = TOK // BLK
ST = BLK // P
QB = SEQ // P
SCALE = float(HD) ** -0.5
EPS = 1e-5
MASKED = -1e30
LEAST = -3e38

STEPS = HEADS // 2 * BATCH
SLOTS = 4
PARTS = 4 * HD
MROW = P - 2


def chunks(n):
    return [(c, min(512, n - c)) for c in range(0, n, 512)]


MAX_UNITS = [(qb, h, c, w) for qb in reversed(range(QB)) for c, w in reversed(chunks((qb + 1) * P))
             for h in range(2)]
UNITS = len(MAX_UNITS)
ST_PAIRS = [(kb, c, max(c * BLK, kb * P), (c + 1) * BLK - max(c * BLK, kb * P))
            for kb in range(QB) for c in range(kb * P // BLK, SEQ // BLK)]
PAIRS_STEP = len(ST_PAIRS)
assert UNITS == 2 * PAIRS_STEP and SLOTS == KT
MAX_BANKS, ST_RING, P_RING = 3, 2, 6
PV_LAG = 2
assert UNITS % MAX_BANKS == 0 and PAIRS_STEP % ST_RING == 0 and PAIRS_STEP % P_RING == 0


def pairs_of(kb):
    return [p for p in range(PAIRS_STEP) if ST_PAIRS[p][0] == kb]


def at_least(engine, sem, value):
    if not isinstance(value, int) or value > 0:
        engine.wait_ge(sem, value)


def for_steps(engine, body):
    for t in range(SLOTS):
        body(t, t)
    with engine.Fori(1, STEPS // SLOTS) as i:
        for j in range(SLOTS):
            body(i * SLOTS + j, j)


class Place:

    def __init__(self, nc, start):
        self.nc, self.at = nc, start

    def __call__(self, name, shape, dt=F32):
        size = 4
        for n in shape[1:]:
            size *= n
        tensor = self.nc.alloc_sbuf_tensor_at(name, shape, dt, offset=self.at)
        self.at += (size + 31) // 32 * 32
        return tensor


def layer_kernel(nc, x, xT, wqT, wkT, wvT, woT, ln_w, gateT, upT, downT, cos, sin, out):
    ctx = ExitStack()
    with ctx:
        def sem(name):
            return ctx.enter_context(nc.semaphore(name))

        qk_dram = nc.dram_tensor("qk_parts", (2, HEADS, 2, HD, TOK), F32, kind="Internal").ap()
        o_dram = nc.dram_tensor("attn_raw", (HEADS, 2 * HD, TOK), F32, kind="Internal").ap()

        BASE = 16 * 1024 + 256
        fixed = Place(nc, BASE)
        ident = fixed("ident", [P, P])
        lnw_sb = fixed("lnw_sb", [P, KT])
        stats = fixed("stats", [P, 2, ST, 6])
        mv1 = fixed("mv1", [P, ST, 2])
        mv2 = fixed("mv2", [P, ST, 2])
        norm_sb = fixed("norm_sb", [P, 7, ST])
        mhalf, var_eps, rstd1, ms_eps, rms, var_eps2, rstd2 = (norm_sb[:, n, :] for n in range(7))
        o_sb = [fixed(f"o_sb{r}", [P, BLK]) for r in range(2)]
        recip = [fixed(f"recip{r}", [P, BLK]) for r in range(2)]
        TOP = 224 * 1024 - 64
        V_AT = TOP - TOK // P * DIM * 4
        v_sb = Place(nc, V_AT)("v_sb", [P, TOK // P, DIM])

        a = Place(nc, fixed.at)
        w_raw = [a(f"w_raw{n}", [P, KT, DIM]) for n in range(3)]
        x_raw = [a(f"x_raw{j}", [P, KT, BLK]) for j in range(2)]
        w_hi = [a(f"w_hi{n}", [P, KT, DIM], F32R) for n in range(3)]
        w_lo = [a(f"w_lo{n}", [P, KT, DIM], F32R) for n in range(3)]
        x_hi = [a(f"x_hi{j}", [P, KT, BLK], F32R) for j in range(2)]
        x_lo = [a(f"x_lo{j}", [P, KT, BLK], F32R) for j in range(2)]
        cos_sb = a("cos_sb", [P, SEQ])
        sin_sb = a("sin_sb", [P, SEQ])
        term = [a(f"term{n}", [P, BLK]) for n in range(4)]
        rot = [a(f"rot{r}", [P, 2, BLK]) for r in range(2)]
        rot_hi = [a(f"rot_hi{r}", [P, 2, BLK], F32R) for r in range(2)]
        rot_lo = [a(f"rot_lo{r}", [P, 2, BLK], F32R) for r in range(2)]
        assert a.at <= V_AT, a.at

        b = Place(nc, fixed.at)
        q_st, k_st = [], []
        q_st.append(b("q_st0", [P, 2, SEQ], F32R))
        k_st.append(b("k_st0", [P, 2, SEQ], F32R))
        q_st.append(b("q_st1", [P, 2, SEQ], F32R))
        assert b.at == fixed.at + 3 * KT * DIM * 4
        SMALL_AT = b.at
        mask = b("mask", [P, BLK])
        v_pair = [b(f"v_pair{r}", [P, QB, 2, 2 * HD]) for r in range(2)]
        row_max = b("row_max", [P, 2, 2, QB])
        m_parts = b("m_parts", [P, 2, 2, QB], F32R)
        m_turned = [b(f"m_turned{s}", [P, 32]) for s in range(SLOTS)]
        K1_AT = b.at
        k_st.append(b("k_st1", [P, 2, SEQ], F32R))
        assert b.at <= fixed.at + (3 + 2) * KT * DIM * 4
        gate_sb = b("gate_sb", [P, KT, INNER])
        up_sb = b("up_sb", [P, KT, INNER])
        MASKED_AT = b.at
        masked = [b(f"masked{n}", [P, BLK]) for n in range(MAX_BANKS + 1)]
        for s in range(2, SLOTS):
            q_st.append(b(f"q_st{s}", [P, 2, SEQ], F32R))
            k_st.append(b(f"k_st{s}", [P, 2, SEQ], F32R))
        probs = b("probs", [P, P_RING, 2, BLK])
        assert b.at <= V_AT, b.at

        early = Place(nc, fixed.at)
        wo_hi = early("wo_hi", [P, KT, DIM], F32R)
        wo_lo = early("wo_lo", [P, KT, DIM], F32R)
        attn_hi = early("attn_hi", [P, KT, BLK], F32R)
        assert early.at <= SMALL_AT
        h_hi = [early(f"h_hi{r}", [P, BLK], F32R) for r in range(2)]
        hid = early("hid", [P, BLK])
        assert early.at <= K1_AT
        attn = Place(nc, K1_AT)("attn", [P, KT, BLK])
        attn_lo = Place(nc, K1_AT)("attn_lo", [P, KT, BLK], F32R)
        norm_tok = attn
        d = Place(nc, MASKED_AT)
        wo_raw = d("res1", [P, ST, DIM])
        res = [d("res0", [P, ST, DIM]), wo_raw]
        nx_hi = [d(f"nx_hi{r}", [P, KT, BLK], F32R) for r in range(2)]
        nx_lo = [d(f"nx_lo{r}", [P, KT, BLK], F32R) for r in range(2)]
        g_hi = [d(f"g_hi{r}", [P, KT, P], F32R) for r in range(2)]
        g_lo = [d(f"g_lo{r}", [P, KT, P], F32R) for r in range(2)]
        u_hi = [d(f"u_hi{r}", [P, KT, P], F32R) for r in range(2)]
        u_lo = [d(f"u_lo{r}", [P, KT, P], F32R) for r in range(2)]
        d_hi = [d(f"d_hi{r}", [P, DIM], F32R) for r in range(2)]
        d_lo = [d(f"d_lo{r}", [P, DIM], F32R) for r in range(2)]
        h_lo = [d(f"h_lo{r}", [P, BLK], F32R) for r in range(2)]
        DOWN_AT = TOP - IT * DIM * 4
        down_sb = Place(nc, DOWN_AT)("down_sb", [P, IT, DIM])
        assert d.at <= DOWN_AT, d.at

        psum = ctx.enter_context(nc.psum_tensor("psum", [P, 8, BLK], F32))
        bank = [psum[:, n, :] for n in range(8)]
        proj_ps = [bank[0:2], bank[2:4]]
        v_ps = bank[4:6]
        max_ps = bank[0:3]
        st_ps = [psum[:, 3 + 2 * n:5 + 2 * n, :] for n in range(ST_RING)]
        o_ps = bank[7]
        y_ps = bank[0:4]
        gate_ps, up_ps = bank[4], bank[5]
        c_ps = bank[6:8]

        tables_in = sem("tables_in")
        first_in = [sem(f"first_in{k}") for k in range(KT)]
        w_in = [None] + [sem(f"w_in{n}") for n in range(1, 3)]
        x_in = [sem(f"x_in{j}") for j in range(2)]
        w_hi_done = sem("w_hi_done")
        w_lo_done = sem("w_lo_done")
        x_hi_done = sem("x_hi_done")
        x_lo_done = sem("x_lo_done")
        proj_done = sem("proj_done")
        proj_free = sem("proj_free")
        term_done = sem("term_done")
        rot_free = sem("rot_free")
        rot_done = sem("rot_done")
        rot_hi_done = sem("rot_hi_done")
        rot_lo_done = sem("rot_lo_done")
        qk_stored = [sem(f"qk_stored{r}") for r in range(2)]
        v_done = sem("v_done")
        v_free = sem("v_free")
        setup_done = sem("setup_done")
        stack_const = sem("stack_const")
        stack_in = [sem(f"stack_in{s}") for s in range(SLOTS)]
        max_scores = sem("max_scores")
        max_taken = sem("max_taken")
        m_step = sem("m_step")
        m_turned_done = sem("m_turned_done")
        m_in = [sem(f"m_in{s}") for s in range(SLOTS)]
        st_scores = sem("st_scores")
        clamped = sem("clamped")
        exp_done = sem("exp_done")
        v_pair_done = sem("v_pair_done")
        causal_done = sem("causal_done")
        pv_done = sem("pv_done")
        o_copied = sem("o_copied")
        o_stored = [sem(f"o_stored{r}") for r in range(2)]
        dve_waited = sem("dve_waited")
        pool_waited = sem("pool_waited")
        ffn_w_in = sem("ffn_w_in")
        down_in = sem("down_in")
        wo_in = sem("wo_in")
        wo_hi_done = sem("wo_hi_done")
        wo_lo_done = sem("wo_lo_done")
        recip_done = sem("recip_done")
        attn_in = [sem(f"attn_in{r}") for r in range(2)]
        res_in = [sem(f"res_in{r}") for r in range(2)]
        attn_scaled = sem("attn_scaled")
        attn_hi_done = sem("attn_hi_done")
        attn_lo_done = sem("attn_lo_done")
        c_done = sem("c_done")
        sum1_done = sem("sum1_done")
        stats_done = sem("stats_done")
        mv1_done = sem("mv1_done")
        pool_step = sem("pool_step")
        rstd1_done = sem("rstd1_done")
        norm1_done = sem("norm1_done")
        norm_tok_done = sem("norm_tok_done")
        turned_done = sem("turned_done")
        nx_hi_done = sem("nx_hi_done")
        nx_lo_done = sem("nx_lo_done")
        gu_hi_done = sem("gu_hi_done")
        gu_lo_done = sem("gu_lo_done")
        gate_done = sem("gate_done")
        up_done = sem("up_done")
        silu_done = sem("silu_done")
        hid_done = sem("hid_done")
        h_hi_done = sem("h_hi_done")
        h_lo_done = sem("h_lo_done")
        d_hi_done = sem("d_hi_done")
        d_lo_done = sem("d_lo_done")
        down_done = sem("down_done")
        sum2_done = sem("sum2_done")
        mv2_done = sem("mv2_done")
        rstd2_done = sem("rstd2_done")
        out_ready = sem("out_ready")
        out_stored = [sem(f"out_stored{r}") for r in range(2)]

        def plain(ap):
            return ap.bitcast(F32)

        def by_tile(dram):
            return dram.rearrange("(k p) n -> p k n", p=P)

        xT_tiles, x_tiles, out_tiles = by_tile(xT), by_tile(x), by_tile(out)
        PAIRS = [(0, 0), (0, 1), (1, 0)]
        FFN_STEPS = IT

        def ffn_done(n, i):
            return n * FFN_STEPS + i + 1

        block = ctx.enter_context(nc.Block())

        @block.sync
        def _(sp):
            for k in range(KT):
                sp.dma_start(w_raw[0][:, k, :], by_tile(wqT)[:, k, :]).then_inc(first_in[k], 16)
                sp.dma_start(x_raw[0][:, k, :], xT_tiles[:, k, 0:BLK]).then_inc(first_in[k], 16)
            sp.dma_start(cos_sb[:], cos.broadcast_to((P, SEQ))).then_inc(tables_in, 16)
            sp.dma_start(sin_sb[:], sin.broadcast_to((P, SEQ))).then_inc(tables_in, 16)
            sp.dma_start(w_raw[1][:], by_tile(wkT)).then_inc(w_in[1], 16)
            sp.dma_start(w_raw[2][:], by_tile(wvT)).then_inc(w_in[2], 16)
            sp.dma_start(x_raw[1][:], xT_tiles[:, :, BLK:2 * BLK]).then_inc(x_in[1], 16)
            sp.dma_start(lnw_sb[:], ln_w).then_inc(tables_in, 16)

            def all_stored(blocks):
                for r in range(2):
                    sp.wait_ge(qk_stored[r], 1 + 16 * 4 * 2 * blocks)

            def load(t, j):
                at_least(sp, st_scores, (t - SLOTS + 1) * PAIRS_STEP)
                if isinstance(t, int) and t < SLOTS:
                    sp.wait_ge(stack_const, 2 * (t + 1))
                s, cols = j % SLOTS, slice(j % 2 * SEQ, j % 2 * SEQ + SEQ)
                for h in range(2):
                    head = (t - j % SLOTS) + j // 2 % 2 * 2 + h if not isinstance(t, int) else t // 2 * 2 + h
                    for part in range(2):
                        src = qk_dram[0, bass.ds(head, 1), part, :, cols].broadcast_to((2, HD, SEQ))
                        sp.dma_start(plain(q_st[s][part * 2 * HD:(part + 1) * 2 * HD, h, :]), src)\
                            .then_inc(stack_in[s], 16)
                    src = qk_dram[1, bass.ds(head, 1), :, :, cols].rearrange("o a r n -> o (a r) n")
                    sp.dma_start(plain(k_st[s][0:PARTS, h, :]), src.broadcast_to((2, 2 * HD, SEQ)))\
                        .then_inc(stack_in[s], 16)

            def place_maxima(t, j):
                sp.wait_ge(m_turned_done, t + 1)
                rows = plain(q_st[j % SLOTS][MROW:MROW + 2, :, :]).rearrange(
                    "p h (g c x) -> p (h g) c x", c=4, x=32)
                for c in range(4):
                    sp.dma_start(rows[:, :, c, :], m_turned[j % SLOTS][32 * c:32 * c + 32, :])\
                        .then_inc(m_in[j % SLOTS], 16)

            def store_output(t, j):
                r = j % 2
                sp.wait_ge(o_copied, t + 1)
                if isinstance(t, int):
                    head = t // 2 * 2
                else:
                    head = (t - j) + j // 2 * 2
                for c in range(2):
                    first = r * SEQ + c * BLK
                    sp.dma_start(o_dram[bass.ds(head, 2), :, first:first + BLK],
                                 o_sb[r][c * 64:(c + 1) * 64, :]).then_inc(o_stored[r], 16)

            for tb in range(NBLK):
                if 1 <= tb < NBLK - 1:
                    sp.wait_ge(x_lo_done, KT * tb)
                    sp.dma_start(x_raw[(tb + 1) % 2][:], xT_tiles[:, :, (tb + 1) * BLK:(tb + 2) * BLK])\
                        .then_inc(x_in[(tb + 1) % 2], 16)
                for g in range(4):
                    if tb == 2 and g == 1:
                        all_stored(2)
                        load(0, 0)
                    sp.wait_ge(rot_lo_done, 4 * tb + g + 1)
                    heads = slice(g % 2 * 16, g % 2 * 16 + 16)
                    for e in range(2):
                        for part, src in enumerate((rot_hi[g % 2], rot_lo[g % 2])):
                            sp.dma_start(qk_dram[g // 2, heads, part, e * HALF:(e + 1) * HALF,
                                                 tb * BLK:(tb + 1) * BLK],
                                         plain(src[:, e, :])).then_inc(qk_stored[g % 2], 16)

            all_stored(NBLK)
            load(1, 1)
            for t in range(SLOTS):
                if t >= 3:
                    store_output(t - 3, t - 3)
                place_maxima(t, t)
                load(t + 2, t + 2)
                sp.dma_start(gate_sb[:, t, :], by_tile(gateT)[:, t, :]).then_inc(ffn_w_in, 16)
            with sp.Fori(1, STEPS // SLOTS - 1) as i:
                for j in range(SLOTS):
                    store_output(i * SLOTS + (j - 3), j - 3)
                    place_maxima(i * SLOTS + j, j)
                    if j < 2:
                        load(i * SLOTS + j + 2, j + 2)
                    else:
                        load(i * SLOTS + SLOTS + j - 2, j - 2)
            for t in range(STEPS - SLOTS, STEPS):
                store_output(t - 3, t - 3)
                place_maxima(t, t)
                if t + 2 < STEPS:
                    load(t + 2, t + 2)
                k = t - (STEPS - SLOTS)
                sp.dma_start(up_sb[:, k, :], by_tile(upT)[:, k, :]).then_inc(ffn_w_in, 16)

            def load_attn(n, k):
                at_least(sp, attn_scaled, n * KT + k - 1)
                if n and k == 0:
                    sp.wait_ge(turned_done, n * KT)
                cols, heads = slice(n * BLK, (n + 1) * BLK), slice(8 * k, 8 * k + 8)
                sp.dma_start(attn[:, k, :], o_dram[heads, 0:HD, cols]).then_inc(attn_in[k % 2], 16)
                sp.dma_start(recip[k % 2][:], o_dram[heads, HD:2 * HD, cols]).then_inc(attn_in[k % 2], 16)

            def load_res(n):
                if n == 1:
                    sp.wait_ge(wo_lo_done, 1)
                if n >= 2:
                    sp.wait_ge(out_stored[n % 2], 16 * (n // 2))
                sp.dma_start(res[n % 2][:], x_tiles[:, n * ST:(n + 1) * ST, :]).then_inc(res_in[n % 2], 16)

            def store(n):
                sp.wait_ge(out_ready, ST * (n + 1))
                sp.dma_start(out_tiles[:, n * ST:(n + 1) * ST, :], res[n % 2][:]).then_inc(out_stored[n % 2], 16)

            sp.wait_ge(max_taken, STEPS * UNITS)
            sp.wait_ge(st_scores, (STEPS - 2) * PAIRS_STEP)
            sp.dma_start(wo_raw[:], by_tile(woT)).then_inc(wo_in, 16)
            sp.wait_ge(o_stored[0], 32 * (STEPS // 2 - 2))
            for k in range(KT - 1):
                load_attn(0, k)
            store_output(STEPS - 3, STEPS - 3)
            sp.wait_ge(v_pair_done, STEPS)
            sp.dma_start(down_sb[:], by_tile(downT)).then_inc(down_in, 16)
            store_output(STEPS - 2, STEPS - 2)
            sp.wait_ge(o_stored[0], 32 * (STEPS // 2))
            load_attn(0, KT - 1)
            sp.wait_ge(pv_done, STEPS * QB)
            load_res(0)
            store_output(STEPS - 1, STEPS - 1)
            sp.wait_ge(o_stored[1], 32 * (STEPS // 2))
            load_res(1)
            for n in range(NBLK):
                if n + 1 < NBLK:
                    load_attn(n + 1, 0)
                    load_attn(n + 1, 1)
                if n >= 1:
                    store(n - 1)
                    if n + 1 < NBLK:
                        load_res(n + 1)
                if n + 1 < NBLK:
                    load_attn(n + 1, 2)
                    load_attn(n + 1, 3)
            store(NBLK - 1)
            for r in range(2):
                sp.wait_ge(out_stored[r], 16 * NBLK // 2)

        @block.gpsimd
        def _(pool):
            pool.sem_inc(proj_free, 2)
            pool.sem_inc(rot_free, 2)
            pool.sem_inc(v_free, 2)
            pool.sem_inc(qk_stored[0], 1)
            pool.sem_inc(qk_stored[1], 1)
            pool.sem_inc(down_done, 1)
            nc.gpsimd.memset(mhalf, -0.5)
            nc.gpsimd.memset(ident[:], 0.0).then_inc(setup_done, 1)
            pool.wait_ge(setup_done, 1)
            nc.gpsimd.affine_select(out=ident[:], in_=ident[:], compare_op=ALU.not_equal, fill=1.0, base=0,
                                    pattern=[[-1, P]], channel_multiplier=1).then_inc(setup_done, 1)

            def stack_constants(stacks):
                for stack in stacks:
                    nc.gpsimd.memset(plain(stack[PARTS:P, :, :]), 0.0 if stack in q_st else 1.0)\
                        .then_inc(stack_const, 1)

            pool.wait_ge(setup_done, 2)
            pool.wait_ge(w_lo_done, KT + 2)
            stack_constants([q_st[0], k_st[0], q_st[1]])
            pool.wait_ge(stack_const, 3)

            with pool.Fori(0, NBLK // 2) as n:
                for j in range(2):
                    for g in range(4):
                        use = n * 8 + j * 4 + g
                        pool.wait_ge(rot_hi_done, use + 1)
                        nc.gpsimd.tensor_tensor(rot_lo[g % 2][:], rot[g % 2][:], plain(rot_hi[g % 2][:]),
                                                ALU.subtract).then_inc(rot_lo_done, 1)
                        pool.wait_ge(rot_lo_done, use + 1)
                        pool.sem_inc(rot_free, 1)

            pool.wait_ge(x_lo_done, KT * NBLK)
            nc.gpsimd.memset(mask[:], 0.0).then_inc(setup_done, 1)
            pool.wait_ge(setup_done, 3)
            nc.gpsimd.affine_select(out=mask[:, BLK - P:BLK], in_=mask[:, BLK - P:BLK], compare_op=ALU.is_ge,
                                    fill=MASKED, base=0, pattern=[[-1, P]], channel_multiplier=1)\
                .then_inc(setup_done, 1)
            pool.wait_ge(setup_done, 4)
            stack_constants([k_st[1]])
            pool.wait_ge(stack_const, 4)
            for r in range(2):
                nc.gpsimd.memset(v_pair[r][:], 1.0).then_inc(setup_done, 1)
            pool.wait_ge(setup_done, 6)
            for r in range(2):
                pool.wait_ge(qk_stored[r], 1 + 16 * 4 * 2 * NBLK)
            pool.wait_ge(v_free, 2 + NBLK * ST)
            stack_constants([q_st[2], k_st[2], q_st[3], k_st[3]])
            pool.wait_ge(stack_const, 2 * SLOTS)

            def step(t, j):
                at_least(pool, pv_done, (t - 1) * QB)
                cols = t // 2 * 2 * HD if isinstance(t, int) else (t - j) * HD + j // 2 * 2 * HD
                src = v_sb[:, j % 2 * QB:(j % 2 + 1) * QB, bass.ds(cols, 2 * HD)]
                nc.gpsimd.tensor_copy(v_pair[j % 2][:, :, :, 0:HD],
                                      src.rearrange("p k (h d) -> p k h d", h=2)).then_inc(v_pair_done, 1)
                for kb in range(QB):
                    p = pairs_of(kb)[0]
                    pool.wait_ge(exp_done, t * PAIRS_STEP + p + 1)
                    pool.sem_inc(pool_waited, 1)
                    p2 = probs[:, p % P_RING, :, 0:P]
                    nc.gpsimd.affine_select(out=p2, in_=p2, compare_op=ALU.is_ge, fill=0.0, base=0,
                                            pattern=[[0, 2], [1, P]], channel_multiplier=-1)\
                        .then_inc(causal_done, 1)

            for_steps(pool, step)

            steps = [0]

            def link(ins):
                steps[0] += 1
                ins.then_inc(pool_step, 1)
                pool.wait_ge(pool_step, steps[0])

            def first_norm(n):
                pool.wait_ge(mv1_done, ST * (n + 1))
                if n:
                    pool.wait_ge(norm_tok_done, ST * n)
                mean_var = mv1[:, :, 1]
                link(nc.gpsimd.tensor_scalar(var_eps, mean_var, EPS, None, ALU.add))
                link(nc.gpsimd.tensor_tensor(rstd1, var_eps, mhalf, ALU.pow))
                link(nc.gpsimd.tensor_tensor(ms_eps, rstd1, rstd1, ALU.mult))
                link(nc.gpsimd.tensor_tensor(ms_eps, ms_eps, mean_var, ALU.mult))
                link(nc.gpsimd.tensor_scalar(ms_eps, ms_eps, EPS, None, ALU.add))
                nc.gpsimd.tensor_tensor(rms, ms_eps, mhalf, ALU.pow).then_inc(rstd1_done, 1)

            def second_norm(n):
                pool.wait_ge(mv2_done, ST * (n + 1))
                if n:
                    pool.wait_ge(out_ready, ST * n)
                link(nc.gpsimd.tensor_scalar(var_eps2, mv2[:, :, 1], EPS, None, ALU.add))
                nc.gpsimd.tensor_tensor(rstd2, var_eps2, mhalf, ALU.pow).then_inc(rstd2_done, 1)

            first_norm(0)
            for n in range(NBLK):
                if n >= 1:
                    second_norm(n - 1)
                if n + 1 < NBLK:
                    first_norm(n + 1)
            second_norm(NBLK - 1)

        @block.scalar
        def _(act):
            def x_hi_of(tb):
                if tb:
                    act.wait_ge(x_in[tb % 2], (tb + 1) // 2 * 16)
                for k in range(KT):
                    nc.scalar.copy(x_hi[tb % 2][:, k, :], x_raw[tb % 2][:, k, :]).then_inc(x_hi_done, 1)

            for k in range(KT):
                act.wait_ge(first_in[k], 32)
                nc.scalar.copy(w_hi[0][:, k, :], w_raw[0][:, k, :]).then_inc(w_hi_done, 1)
                nc.scalar.copy(x_hi[0][:, k, :], x_raw[0][:, k, :]).then_inc(x_hi_done, 1)
            for n in range(1, 3):
                act.wait_ge(w_in[n], 16)
                nc.scalar.copy(w_hi[n][:], w_raw[n][:]).then_inc(w_hi_done, 1)
            for tb in range(NBLK):
                for g in range(4):
                    act.wait_ge(rot_done, tb * 4 + g + 1)
                    act.wait_ge(qk_stored[g % 2], tb * 128 + g // 2 * 64 + 1)
                    nc.scalar.copy(rot_hi[g % 2][:], rot[g % 2][:]).then_inc(rot_hi_done, 1)
                    if g == 0 and tb + 1 < NBLK:
                        x_hi_of(tb + 1)
                for s in range(ST):
                    act.wait_ge(v_done, tb * ST + s + 1)
                    nc.scalar.copy(v_sb[:, tb * ST + s, :], v_ps[s % 2]).then_inc(v_free, 1)

            def exps(t, first, last):
                for p in range(first, last):
                    kb, c, q0, w = ST_PAIRS[p]
                    scores, to = st_ps[p % ST_RING], probs[:, p % P_RING]
                    act.wait_ge(st_scores, t * PAIRS_STEP + p + 1)
                    skip = P if w == P else 0
                    diagonal = q0 == kb * P
                    if diagonal:
                        square = scores[:, :, skip:skip + P]
                        nc.scalar.activation(square, square, ACT.Relu, scale=-1.0).then_inc(clamped, 1)
                    before = ST_PAIRS[(p - P_RING) % PAIRS_STEP][0]
                    at_least(act, pv_done, (t if p >= P_RING else t - 1) * QB + before + 1)
                    if diagonal:
                        if w > P:
                            nc.scalar.activation(to[:, :, P:w], scores[:, :, P:w], ACT.Exp, scale=SCALE)
                        act.wait_ge(clamped, t * QB + kb + 1)
                        nc.scalar.activation(to[:, :, 0:P], square, ACT.Exp, scale=-SCALE).then_inc(exp_done, 1)
                    else:
                        nc.scalar.activation(to, scores, ACT.Exp, scale=SCALE).then_inc(exp_done, 1)

            def output(t, j):
                act.wait_ge(pv_done, t * QB)
                r = (j - 1) % 2
                if isinstance(t, int):
                    at_least(act, o_stored[r], (t - 1) // 2 * 32)
                else:
                    act.wait_ge(o_stored[r], (t - j) * 16 + (j - 1) // 2 * 32)
                nc.scalar.copy(o_sb[r][:], o_ps).then_inc(o_copied, 1)

            def step(t, j):
                exps(t, 0, PV_LAG)
                if not (isinstance(t, int) and t == 0):
                    output(t, j)
                exps(t, PV_LAG, PAIRS_STEP)

            for_steps(act, step)
            output(STEPS, STEPS)

            def attn_part(n, k):
                act.wait_ge(attn_scaled, n * KT + k + 1)
                if isinstance(k, int):
                    src, to = attn[:, k, :], attn_hi[:, k, :]
                else:
                    src, to = attn[:, bass.ds(k, 1), :], attn_hi[:, bass.ds(k, 1), :]
                nc.scalar.copy(to, src).then_inc(attn_hi_done, 1)

            def turned_parts(n, ks):
                at_least(act, up_done, (n - 1) * FFN_STEPS)
                for k in ks:
                    act.wait_ge(turned_done, n * KT + k + 1)
                    nc.scalar.activation(nx_hi[n % 2][:, k, :], c_ps[k % 2], ACT.Copy,
                                         scale=lnw_sb[:, k:k + 1]).then_inc(nx_hi_done, 1)

            def gate_up_hi(n, i, r):
                at_least(act, up_done, n * FFN_STEPS + i - 1)
                cols = slice(i * P, (i + 1) * P) if isinstance(i, int) else bass.ds(i * P, P)
                nc.scalar.copy(g_hi[r][:], gate_sb[:, :, cols]).then_inc(gu_hi_done, 1)
                nc.scalar.copy(u_hi[r][:], up_sb[:, :, cols]).then_inc(gu_hi_done, 1)

            def silu_of(n, i, r):
                act.wait_ge(gate_done, n * FFN_STEPS + i + 1)
                at_least(act, h_lo_done, n * FFN_STEPS + i)
                nc.scalar.activation(hid[:], gate_ps, ACT.Silu).then_inc(silu_done, 1)
                at_least(act, down_done, n * FFN_STEPS + i)
                src = down_sb[:, i, :] if isinstance(i, int) else \
                    down_sb[:, bass.ds(i, 1), :].rearrange("p o n -> p (o n)")
                nc.scalar.copy(d_hi[r][:], src).then_inc(d_hi_done, 1)

            def ffn_step(n, i, r):
                gate_up_hi(n, i, r)
                silu_of(n, i - 1, 1 - r)

            def ffn_steps(n, first, last):
                with act.Fori(first // 2, last // 2) as i:
                    for r in range(2):
                        ffn_step(n, i * 2 + r, r)

            act.wait_ge(ffn_w_in, 32 * KT)
            gate_up_hi(0, 0, 0)
            act.wait_ge(down_in, 16)
            turned_parts(0, range(KT))
            for n in range(NBLK):
                if n >= 1:
                    gate_up_hi(n, 0, 0)
                    silu_of(n - 1, IT - 1, 1)
                ffn_step(n, 1, 1)
                ffn_steps(n, 2, 4)
                if n + 1 == NBLK:
                    ffn_steps(n, 4, IT)
                    continue
                with act.Fori(2, 4) as i:
                    for r in range(2):
                        ffn_step(n, i * 2 + r, r)
                        if r == 0:
                            act.wait_ge(c_done, (n + 1) * ST)
                        attn_part(n + 1, i * 2 + (r - 4))
                ffn_steps(n, 8, 10)
                for r in range(2):
                    ffn_step(n, 10 + r, r)
                    turned_parts(n + 1, (2 * r, 2 * r + 1))
                ffn_steps(n, 12, IT)
            silu_of(NBLK - 1, IT - 1, 1)

        @block.vector
        def _(dve):
            def x_lo_of(tb, ks):
                for k in ks:
                    dve.wait_ge(x_hi_done, tb * KT + k + 1)
                    nc.vector.tensor_tensor(x_lo[tb % 2][:, k, :], x_raw[tb % 2][:, k, :],
                                            plain(x_hi[tb % 2][:, k, :]), ALU.subtract).then_inc(x_lo_done, 1)

            for k in range(KT):
                dve.wait_ge(w_hi_done, k + 1)
                nc.vector.tensor_tensor(w_lo[0][:, k, :], w_raw[0][:, k, :], plain(w_hi[0][:, k, :]),
                                        ALU.subtract).then_inc(w_lo_done, 1)
                x_lo_of(0, (k,))
            for n in range(1, 3):
                dve.wait_ge(w_hi_done, KT + n)
                nc.vector.tensor_tensor(w_lo[n][:], w_raw[n][:], plain(w_hi[n][:]), ALU.subtract)\
                    .then_inc(w_lo_done, 1)
            dve.wait_ge(tables_in, 48)
            for tb in range(NBLK):
                cos_j, sin_j = (t[:, tb % 2 * BLK:(tb % 2 + 1) * BLK] for t in (cos_sb, sin_sb))
                for g in range(4):
                    use = tb * 4 + g
                    even, odd = proj_ps[g % 2]
                    dve.wait_ge(proj_done, use + 1)
                    nc.vector.tensor_tensor(term[0][:], even, cos_j, ALU.mult)
                    nc.vector.tensor_tensor(term[1][:], odd, sin_j, ALU.mult)
                    nc.vector.tensor_tensor(term[2][:], even, sin_j, ALU.mult)
                    nc.vector.tensor_tensor(term[3][:], odd, cos_j, ALU.mult).then_inc(term_done, 1)
                    dve.wait_ge(term_done, use + 1)
                    dve.sem_inc(proj_free, 1)
                    dve.wait_ge(rot_free, use + 1)
                    nc.vector.tensor_tensor(rot[g % 2][:, 0, :], term[0][:], term[1][:], ALU.subtract)
                    nc.vector.tensor_tensor(rot[g % 2][:, 1, :], term[2][:], term[3][:], ALU.add)\
                        .then_inc(rot_done, 1)
                    dve.wait_ge(rot_done, use + 1)
                    if 1 <= g < 3 and tb + 1 < NBLK:
                        x_lo_of(tb + 1, (2 * g - 2, 2 * g - 1))

            dve.wait_ge(setup_done, 4)

            def step(t, j):
                for u, (qb, h, c, w) in enumerate(MAX_UNITS):
                    diagonal = c + w == (qb + 1) * P
                    dve.wait_ge(max_scores, t * UNITS + u + 1)
                    if diagonal:
                        dve.sem_inc(dve_waited, 1)
                    scores = max_ps[u % MAX_BANKS][:, 0:w]
                    to = row_max[:, c // BLK, h, qb:qb + 1]
                    if diagonal:
                        nc.vector.tensor_tensor_reduce(masked[u % (MAX_BANKS + 1)][:, 0:w], scores, mask[:, BLK - w:BLK], 1.0, LEAST,
                                                       ALU.add, ALU.max, to).then_inc(max_taken, 1)
                    else:
                        nc.vector.tensor_reduce(to, scores, AX.X, ALU.max).then_inc(max_taken, 1)
                dve.wait_ge(max_taken, (t + 1) * UNITS)
                late = row_max[:, 0, :, QB // 2:QB]
                nc.vector.tensor_tensor(late, late, row_max[:, 1, :, QB // 2:QB], ALU.max).then_inc(m_step, 1)
                dve.wait_ge(m_step, t * 3 + 1)
                at_least(dve, m_turned_done, t)
                nc.vector.tensor_scalar(m_parts[:, 0], row_max[:, 0], -1.0, None, ALU.mult).then_inc(m_step, 1)
                dve.wait_ge(m_step, t * 3 + 2)
                nc.vector.scalar_tensor_tensor(m_parts[:, 1], row_max[:, 0], -1.0, plain(m_parts[:, 0]),
                                               ALU.mult, ALU.subtract).then_inc(m_step, 1)
                dve.wait_ge(m_step, t * 3 + 3)
                if isinstance(t, int):
                    at_least(dve, m_in[j % SLOTS], t // SLOTS * 64)
                else:
                    dve.wait_ge(m_in[j % SLOTS], (t - j) * 16)
                nc.vector.transpose(m_turned[j % SLOTS][:], plain(m_parts[:].rearrange("p a h q -> p (a h q)")))\
                    .then_inc(m_turned_done, 1)

            for_steps(dve, step)

            def attn_scale(n, k, r):
                use = n * KT + k
                if isinstance(k, int):
                    dve.wait_ge(attn_in[r], 32 * (n * KT // 2 + k // 2 + 1))
                    to = attn[:, k, :]
                else:
                    dve.wait_ge(attn_in[r], k * 16 + (n * KT // 2 * 32 - r * 16 + 32))
                    to = attn[:, bass.ds(k, 1), :].rearrange("p o n -> p (o n)")
                nc.vector.reciprocal(recip[r][:], recip[r][:]).then_inc(recip_done, 1)
                dve.wait_ge(recip_done, use + 1)
                nc.vector.tensor_tensor(to, to, recip[r][:], ALU.mult).then_inc(attn_scaled, 1)

            def attn_part(n, k):
                dve.wait_ge(attn_hi_done, n * KT + k + 1)
                if isinstance(k, int):
                    lo, src, hi = attn_lo[:, k, :], attn[:, k, :], plain(attn_hi[:, k, :])
                else:
                    at = bass.ds(k, 1)
                    lo, src, hi = attn_lo[:, at, :], attn[:, at, :], plain(attn_hi[:, at, :])
                nc.vector.tensor_tensor(lo, src, hi, ALU.subtract).then_inc(attn_lo_done, 1)

            def tile_stats(src, parts, to, done):
                nc.vector.bn_stats(parts, src).then_inc(stats_done, 1)
                seen[0] += 1
                dve.wait_ge(stats_done, seen[0])
                nc.vector.bn_aggr(to, parts).then_inc(done, 1)

            seen = [0]

            def first_sum(n):
                dve.wait_ge(res_in[n % 2], 16 * (n // 2 + 1))
                if n:
                    dve.wait_ge(rstd1_done, n)
                    dve.wait_ge(norm1_done, ST * n)
                for s in range(ST):
                    z = res[n % 2][:, s, :]
                    dve.wait_ge(c_done, n * ST + s + 1)
                    nc.vector.tensor_tensor(z, c_ps[s % 2], z, ALU.add).then_inc(sum1_done, 1)
                    dve.wait_ge(sum1_done, n * ST + s + 1)
                    tile_stats(z, stats[:, 0, s, :], mv1[:, s, :], mv1_done)

            def first_norm(n):
                dve.wait_ge(rstd1_done, n + 1)
                for s in range(ST):
                    z = res[n % 2][:, s, :]
                    nc.vector.tensor_scalar(z, z, mv1[:, s, 0:1], rstd1[:, s:s + 1], ALU.subtract, ALU.mult)\
                        .then_inc(norm1_done, 1)
                for s in range(ST):
                    dve.wait_ge(norm1_done, n * ST + s + 1)
                    nc.vector.tensor_scalar(norm_tok[:, s, :], res[n % 2][:, s, :], rms[:, s:s + 1], None,
                                            ALU.mult).then_inc(norm_tok_done, 1)

            def turned_parts(n, ks):
                for k in ks:
                    dve.wait_ge(nx_hi_done, n * KT + k + 1)
                    nc.vector.scalar_tensor_tensor(nx_lo[n % 2][:, k, :], c_ps[k % 2], lnw_sb[:, k:k + 1],
                                                   plain(nx_hi[n % 2][:, k, :]), ALU.mult, ALU.subtract)\
                        .then_inc(nx_lo_done, 1)

            def gate_up_lo(n, i, r):
                done = (n * FFN_STEPS + i) * 2
                cols = slice(i * P, (i + 1) * P) if isinstance(i, int) else bass.ds(i * P, P)
                dve.wait_ge(gu_hi_done, done + 1)
                nc.vector.tensor_tensor(g_lo[r][:], gate_sb[:, :, cols], plain(g_hi[r][:]), ALU.subtract)\
                    .then_inc(gu_lo_done, 1)
                dve.wait_ge(gu_hi_done, done + 2)
                nc.vector.tensor_tensor(u_lo[r][:], up_sb[:, :, cols], plain(u_hi[r][:]), ALU.subtract)\
                    .then_inc(gu_lo_done, 1)

            def hidden(n, i, r):
                done = n * FFN_STEPS + i
                dve.wait_ge(silu_done, done + 1)
                dve.wait_ge(up_done, done + 1)
                nc.vector.tensor_tensor(hid[:], up_ps, hid[:], ALU.mult).then_inc(hid_done, 1)
                dve.wait_ge(hid_done, done + 1)
                at_least(dve, down_done, done)
                nc.vector.tensor_copy(h_hi[r][:], hid[:]).then_inc(h_hi_done, 1)
                dve.wait_ge(h_hi_done, done + 1)
                nc.vector.tensor_tensor(h_lo[r][:], hid[:], plain(h_hi[r][:]), ALU.subtract)\
                    .then_inc(h_lo_done, 1)
                dve.wait_ge(d_hi_done, done + 1)
                src = down_sb[:, i, :] if isinstance(i, int) else \
                    down_sb[:, bass.ds(i, 1), :].rearrange("p o n -> p (o n)")
                nc.vector.tensor_tensor(d_lo[r][:], src, plain(d_hi[r][:]), ALU.subtract).then_inc(d_lo_done, 1)

            def second_sum(n):
                dve.wait_ge(down_done, 1 + ffn_done(n, IT - 1))
                for s in range(ST):
                    z = res[n % 2][:, s, :]
                    nc.vector.tensor_tensor(z, y_ps[s], z, ALU.add).then_inc(sum2_done, 1)

            def second_stats(n):
                if n:
                    dve.wait_ge(rstd2_done, n)
                    dve.wait_ge(out_ready, ST * n)
                for s in range(ST):
                    dve.wait_ge(sum2_done, n * ST + s + 1)
                    tile_stats(res[n % 2][:, s, :], stats[:, 1, s, :], mv2[:, s, :], mv2_done)

            def second_norm(n):
                dve.wait_ge(rstd2_done, n + 1)
                for s in range(ST):
                    z = res[n % 2][:, s, :]
                    nc.vector.tensor_scalar(z, z, mv2[:, s, 0:1], rstd2[:, s:s + 1], ALU.subtract, ALU.mult)\
                        .then_inc(out_ready, 1)

            def ffn_step(n, i, r):
                gate_up_lo(n, i, r)
                hidden(n, i - 1, 1 - r)

            def ffn_steps(n, first, last):
                with dve.Fori(first // 2, last // 2) as i:
                    for r in range(2):
                        ffn_step(n, i * 2 + r, r)

            dve.wait_ge(wo_in, 16)
            nc.vector.tensor_copy(wo_hi[:], wo_raw[:]).then_inc(wo_hi_done, 1)
            dve.wait_ge(wo_hi_done, 1)
            nc.vector.tensor_tensor(wo_lo[:], wo_raw[:], plain(wo_hi[:]), ALU.subtract).then_inc(wo_lo_done, 1)
            for k in range(KT):
                attn_scale(0, k, k % 2)
                dve.wait_ge(attn_scaled, k + 1)
                nc.vector.tensor_copy(attn_hi[:, k, :], attn[:, k, :]).then_inc(attn_hi_done, 1)
                attn_part(0, k)
            first_sum(0)
            first_norm(0)
            dve.wait_ge(ffn_w_in, 32 * KT)
            dve.wait_ge(down_in, 16)
            gate_up_lo(0, 0, 0)
            turned_parts(0, range(KT))
            for n in range(NBLK):
                if n >= 1:
                    gate_up_lo(n, 0, 0)
                    hidden(n - 1, IT - 1, 1)
                gate_up_lo(n, 1, 1)
                if n >= 1:
                    second_sum(n - 1)
                hidden(n, 0, 0)
                if n >= 1:
                    second_stats(n - 1)
                ffn_steps(n, 2, 4)
                if n >= 1:
                    second_norm(n - 1)
                if n + 1 == NBLK:
                    ffn_steps(n, 4, IT)
                    continue
                with dve.Fori(2, 4) as i:
                    for r in range(2):
                        ffn_step(n, i * 2 + r, r)
                        k = i * 2 + (r - 4)
                        attn_scale(n + 1, k, r)
                        attn_part(n + 1, k)
                ffn_step(n, 8, 0)
                first_sum(n + 1)
                ffn_step(n, 9, 1)
                first_norm(n + 1)
                for r in range(2):
                    ffn_step(n, 10 + r, r)
                    turned_parts(n + 1, (2 * r, 2 * r + 1))
                ffn_steps(n, 12, IT)
            hidden(NBLK - 1, IT - 1, 1)
            second_sum(NBLK - 1)
            second_stats(NBLK - 1)
            second_norm(NBLK - 1)

        @block.tensor
        def _(pe):
            def product(to, left, right, first=True, last=True):
                for n, (a_, b_) in enumerate(PAIRS):
                    mm = nc.tensor.matmul(to, left[a_], right[b_], start=first and n == 0,
                                          stop=last and n == len(PAIRS) - 1)
                return mm

            with pe.Fori(0, NBLK // 2) as n:
                for j in range(2):
                    for g in range(4):
                        use = n * 8 + j * 4 + g
                        w = g // 2
                        if w:
                            pe.wait_ge(w_lo_done, KT + w)
                        pe.wait_ge(proj_free, use + 1)
                        for half in range(2):
                            cols = slice((g % 2 * 2 + half) * P, (g % 2 * 2 + half + 1) * P)
                            for k in range(KT):
                                if g == 0 and half == 0:
                                    pe.wait_ge(w_lo_done, k + 1)
                                    pe.wait_ge(x_lo_done, n * 8 + j * 4 + k + 1)
                                mm = product(proj_ps[g % 2][half],
                                             (w_hi[w][:, k, cols], w_lo[w][:, k, cols]),
                                             (x_hi[j][:, k, :], x_lo[j][:, k, :]), k == 0, k == KT - 1)
                        mm.then_inc(proj_done, 1)
                    for s in range(ST):
                        pe.wait_ge(w_lo_done, KT + 2)
                        pe.wait_ge(v_free, n * 8 + j * 4 + s + 1)
                        rows = slice(s * P, (s + 1) * P)
                        for k in range(KT):
                            mm = product(v_ps[s % 2], (x_hi[j][:, k, rows], x_lo[j][:, k, rows]),
                                         (w_hi[2][:, k, :], w_lo[2][:, k, :]), k == 0, k == KT - 1)
                        mm.then_inc(v_done, 1)

            pe.wait_ge(rot_done, 4 * NBLK)
            pe.wait_ge(v_free, 2 + NBLK * ST)

            def max_scores_of(t, j, p):
                s = j % SLOTS
                for u in (2 * p, 2 * p + 1):
                    qb, h, c, w = MAX_UNITS[u]
                    at_least(pe, max_taken, t * UNITS + u + 1 - MAX_BANKS)
                    wide = max(w, 2 * P)
                    nc.tensor.matmul(max_ps[u % MAX_BANKS][:, 0:wide],
                                     q_st[s][0:MROW, h, qb * P:(qb + 1) * P],
                                     k_st[s][0:MROW, h, c:c + wide], start=True, stop=True)\
                        .then_inc(max_scores, 1)

            def st_scores_of(t, j, p):
                s = j % SLOTS
                kb, c, q0, w = ST_PAIRS[p]
                at_least(pe, exp_done, t * PAIRS_STEP + p + 1 - ST_RING)
                wide = max(w, 2 * P)
                q0 -= wide - w
                for h in range(2):
                    mm = nc.tensor.matmul(st_ps[p % ST_RING][:, h, 0:wide],
                                          k_st[s][:, h, kb * P:(kb + 1) * P],
                                          q_st[s][:, h, q0:q0 + wide], start=True, stop=True)
                mm.then_inc(st_scores, 1)

            def values(t, j, kb):
                pe.wait_ge(exp_done, t * PAIRS_STEP + pairs_of(kb)[-1] + 1)
                pe.wait_ge(causal_done, t * QB + kb + 1)
                if kb == 0:
                    pe.wait_ge(v_pair_done, t + 1)
                    at_least(pe, o_copied, t)
                for p in pairs_of(kb):
                    _, c, q0, w = ST_PAIRS[p]
                    for h in range(2):
                        rows = (c * 2 + h) * 32
                        mm = nc.tensor.matmul(o_ps[rows:rows + 2 * HD, q0 - c * BLK:q0 - c * BLK + w],
                                              v_pair[j % 2][:, kb, h, :], probs[:, p % P_RING, h, 0:w],
                                              start=kb == 0, stop=kb == (c + 1) * BLK // P - 1)
                mm.then_inc(pv_done, 1)

            def step(t, j, maxima=True, late=True, last=True):
                fixed_t = isinstance(t, int)
                if maxima:
                    s = j % SLOTS
                    pe.wait_ge(stack_in[s], t // SLOTS * 96 + 96 if fixed_t else (t - j) * 24 + 96)
                s2 = (j - 2) % SLOTS
                if late:
                    uses = (t - 2) // SLOTS * 64 + 64 if fixed_t else (t - j) * 16 + (j - 2) // SLOTS * 64 + 64
                    pe.wait_ge(m_in[s2], uses)
                for p in range(PAIRS_STEP):
                    if late:
                        st_scores_of(t - 2, s2, p)
                    if maxima:
                        max_scores_of(t, j, p)
                    behind = (p - PV_LAG) % PAIRS_STEP
                    kb = ST_PAIRS[behind][0]
                    if pairs_of(kb)[-1] != behind:
                        continue
                    if p >= PV_LAG and late:
                        values(t - 2, s2, kb)
                    elif p < PV_LAG and (not fixed_t or t >= 3):
                        values(t - 3, (j - 3) % SLOTS, kb)

            for t in range(SLOTS):
                step(t, t, late=t >= 2)
            with pe.Fori(1, STEPS // SLOTS) as i:
                for j in range(SLOTS):
                    step(i * SLOTS + j, j)
            for t in range(STEPS, STEPS + 2):
                step(t, t, maxima=False)
            for kb in range(QB - PV_LAG, QB):
                values(STEPS - 1, (STEPS - 1) % SLOTS, kb)

            pe.wait_ge(o_copied, STEPS)
            pe.wait_ge(wo_lo_done, 1)

            def project(n):
                for s in range(ST):
                    rows = slice(s * P, (s + 1) * P)
                    at_least(pe, sum1_done, n * ST + s - 1)
                    for k in range(KT):
                        if s == 0:
                            pe.wait_ge(attn_lo_done, n * KT + k + 1)
                        mm = product(c_ps[s % 2], (attn_hi[:, k, rows], attn_lo[:, k, rows]),
                                     (wo_hi[:, k, :], wo_lo[:, k, :]), k == 0, k == KT - 1)
                    mm.then_inc(c_done, 1)

            def turn(n, ks):
                for k in ks:
                    at_least(pe, nx_lo_done, n * KT + k - 1 if k >= 2 else 0)
                    for s in range(ST):
                        if k == 0:
                            pe.wait_ge(norm_tok_done, n * ST + s + 1)
                        mm = nc.tensor.transpose(c_ps[k % 2][:, s * P:(s + 1) * P],
                                                 norm_tok[:, s, k * P:(k + 1) * P], ident[:])
                    mm.then_inc(turned_done, 1)

            def gate_up(n, i, r):
                done = n * FFN_STEPS + i
                for which, (hi, lo, to, ready, used) in enumerate((
                        (g_hi[r], g_lo[r], gate_ps, gate_done, silu_done),
                        (u_hi[r], u_lo[r], up_ps, up_done, hid_done))):
                    pe.wait_ge(gu_lo_done, done * 2 + which + 1)
                    at_least(pe, used, done)
                    for k in range(KT):
                        if isinstance(i, int) and i == 0 and which == 0:
                            pe.wait_ge(nx_lo_done, n * KT + k + 1)
                        mm = product(to, (hi[:, k, :], lo[:, k, :]),
                                     (nx_hi[n % 2][:, k, :], nx_lo[n % 2][:, k, :]), k == 0, k == KT - 1)
                    mm.then_inc(ready, 1)

            def down(n, i, r, first=False, last=False):
                done = n * FFN_STEPS + i
                pe.wait_ge(h_lo_done, done + 1)
                pe.wait_ge(d_lo_done, done + 1)
                if first:
                    at_least(pe, sum2_done, n * ST)
                for s in range(ST):
                    rows = slice(s * P, (s + 1) * P)
                    mm = product(y_ps[s], (h_hi[r][:, rows], h_lo[r][:, rows]), (d_hi[r][:], d_lo[r][:]),
                                 first, last)
                mm.then_inc(down_done, 1)

            def ffn_step(n, i, r):
                gate_up(n, i, r)
                down(n, i - 1, 1 - r)

            def ffn_steps(n, first, last):
                with pe.Fori(first // 2, last // 2) as i:
                    for r in range(2):
                        ffn_step(n, i * 2 + r, r)

            pe.wait_ge(setup_done, 2)
            project(0)
            turn(0, range(KT))
            gate_up(0, 0, 0)
            for n in range(NBLK):
                if n >= 1:
                    gate_up(n, 0, 0)
                    down(n - 1, IT - 1, 1, last=True)
                gate_up(n, 1, 1)
                down(n, 0, 0, first=True)
                if n + 1 == NBLK:
                    ffn_steps(n, 2, IT)
                    continue
                ffn_steps(n, 2, 8)
                project(n + 1)
                ffn_steps(n, 8, 10)
                for r in range(2):
                    ffn_step(n, 10 + r, r)
                    turn(n + 1, (2 * r, 2 * r + 1))
                ffn_steps(n, 12, IT)
            down(NBLK - 1, IT - 1, 1, last=True)


def kernel(L0_attn_x, L0_attn_wq, L0_attn_wk, L0_attn_wv, L0_attn_wo, L0_ffn_ln_w, L0_ffn_gate_w,
           L0_ffn_up_w, L0_ffn_down_w):
    import numpy as np
    import concourse.bacc as bacc
    from concourse.bass_utils import run_bass_kernel_spmd

    def turned(w):
        return np.ascontiguousarray(np.asarray(w).T)

    def rotary_rows(w):
        w = np.asarray(w).reshape(2, HEADS // 2, HALF, 2, DIM)
        return turned(w.transpose(0, 3, 1, 2, 4).reshape(DIM, DIM))

    position = np.arange(SEQ, dtype=np.float64)
    x = np.ascontiguousarray(np.asarray(L0_attn_x).reshape(TOK, DIM))
    arrays = {
        "x": x,
        "xT": turned(x),
        "wqT": rotary_rows(L0_attn_wq),
        "wkT": rotary_rows(L0_attn_wk),
        "wvT": turned(L0_attn_wv),
        "woT": turned(L0_attn_wo),
        "ln_w": turned(np.asarray(L0_ffn_ln_w).reshape(KT, P)),
        "gateT": turned(L0_ffn_gate_w),
        "upT": turned(L0_ffn_up_w),
        "downT": turned(L0_ffn_down_w),
        "cos": np.cos(position).astype(np.float32).reshape(1, SEQ),
        "sin": np.sin(position).astype(np.float32).reshape(1, SEQ),
    }
    nc = bacc.Bacc("TRN2", target_bir_lowering=False, num_devices=1)
    args = {name: nc.dram_tensor(name, a.shape, mybir.dt.from_np(a.dtype), kind="ExternalInput").ap()
            for name, a in arrays.items()}
    out = nc.dram_tensor("out", (TOK, DIM), F32, kind="ExternalOutput").ap()
    layer_kernel(nc, **args, out=out)
    result = run_bass_kernel_spmd(nc, [arrays], core_ids=[0])
    return result.results[0]["out"].reshape(BATCH, SEQ, DIM)
```

```python
from contextlib import ExitStack

import concourse.bass as bass
from concourse import mybir

F32 = mybir.dt.float32
F32R = mybir.dt.float32r
ALU = mybir.AluOpType
ACT = mybir.ActivationFunctionType
AX = mybir.AxisListType

P = 128
BATCH, SEQ, DIM = 2, 1024, 512
TOK = BATCH * SEQ
HEADS = 32
HD = DIM // HEADS
HALF = HD // 2
INNER = 1792
KT = DIM // P
IT = INNER // P
BLK = 512
NBLK = TOK // BLK
ST = BLK // P
QB = SEQ // P
SCALE = float(HD) ** -0.5
EPS = 1e-5
MASKED = -1e30
LEAST = -3e38

PAIRS_BATCH = HEADS // 2
STEPS = PAIRS_BATCH * BATCH
SLOTS = 4
PARTS = 4 * HD
MROW = P - 2


def chunks(n):
    return [(c, min(512, n - c)) for c in range(0, n, 512)]


MAX_UNITS = [(qb, h, c, w) for qb in reversed(range(QB)) for c, w in reversed(chunks((qb + 1) * P))
             for h in range(2)]
UNITS = len(MAX_UNITS)
ST_PAIRS = [(kb, c, max(c * BLK, kb * P), (c + 1) * BLK - max(c * BLK, kb * P))
            for kb in range(QB) for c in range(kb * P // BLK, SEQ // BLK)]
PAIRS_STEP = len(ST_PAIRS)
assert UNITS == 2 * PAIRS_STEP and SLOTS == KT
MAX_BANKS, ST_RING, P_RING = 3, 2, 6
PV_LAG = 2
assert UNITS % MAX_BANKS == 0 and PAIRS_STEP % ST_RING == 0 and PAIRS_STEP % P_RING == 0


def pairs_of(kb):
    return [p for p in range(PAIRS_STEP) if ST_PAIRS[p][0] == kb]


def at_least(engine, sem, value):
    if not isinstance(value, int) or value > 0:
        engine.wait_ge(sem, value)


def for_steps(engine, body):
    for t in range(SLOTS):
        body(t, t)
    with engine.Fori(1, STEPS // SLOTS) as i:
        for j in range(SLOTS):
            body(i * SLOTS + j, j)


class Place:

    def __init__(self, nc, start):
        self.nc, self.at = nc, start

    def __call__(self, name, shape, dt=F32):
        size = 4
        for n in shape[1:]:
            size *= n
        tensor = self.nc.alloc_sbuf_tensor_at(name, shape, dt, offset=self.at)
        self.at += (size + 31) // 32 * 32
        return tensor


def layer_kernel(nc, x, xT, wqT, wkT, wvT, woT, ln_w, gateT, upT, downT, cos, sin, out):
    ctx = ExitStack()
    with ctx:
        def sem(name):
            return ctx.enter_context(nc.semaphore(name))

        qk_dram = nc.dram_tensor("qk_parts", (2, BATCH, HEADS, 2, HD, SEQ), F32, kind="Internal").ap()
        o_dram = nc.dram_tensor("attn_raw", (BATCH, HEADS, 2 * HD, SEQ), F32, kind="Internal").ap()
        r_dram = nc.dram_tensor("sum_recip", (BATCH, HEADS, SEQ), F32, kind="Internal").ap()
        qk_steps = qk_dram.rearrange("w b h a d n -> w (b h) a d n")
        o_steps = o_dram.rearrange("b h d n -> (b h) d n")

        BASE = 16 * 1024 + 256
        fixed = Place(nc, BASE)
        ident = fixed("ident", [P, P])
        lnw_sb = fixed("lnw_sb", [P, KT])
        row_max = [None, Place(nc, fixed.at)("row_max1", [P, 2, 2, QB])]
        stats = fixed("stats", [P, 2, ST, 6])
        mv1 = fixed("mv1", [P, ST, 2])
        mv2 = fixed("mv2", [P, ST, 2])
        norm_sb = fixed("norm_sb", [P, 7, ST])
        mhalf, var_eps, rstd1, ms_eps, rms, var_eps2, rstd2 = (norm_sb[:, n, :] for n in range(7))
        o_sb = [fixed(f"o_sb{r}", [P, BLK]) for r in range(2)]
        recip = [fixed(f"recip{r}", [P, BLK]) for r in range(2)]
        SUMS = HEADS * SEQ // P
        sums = recip[0][:, 0:SUMS]
        TOP = 224 * 1024 - 64
        V_AT = TOP - TOK // P * DIM * 4
        v_sb = Place(nc, V_AT)("v_sb", [P, STEPS, QB, 2 * HD])

        a = Place(nc, fixed.at)
        w_raw = [a(f"w_raw{n}", [P, KT, DIM]) for n in range(3)]
        x_raw = [a(f"x_raw{j}", [P, KT, BLK]) for j in range(2)]
        w_hi = [a(f"w_hi{n}", [P, KT, DIM], F32R) for n in range(3)]
        w_lo = [a(f"w_lo{n}", [P, KT, DIM], F32R) for n in range(3)]
        OWN_AT = a.at
        term = [a(f"term{n}", [P, BLK]) for n in range(4)]
        cos_sb = a("cos_sb", [P, SEQ])
        sin_sb = a("sin_sb", [P, SEQ])
        OWN_END = a.at
        x_hi = [a(f"x_hi{j}", [P, KT, BLK], F32R) for j in range(2)]
        x_lo = [a(f"x_lo{j}", [P, KT, BLK], F32R) for j in range(2)]
        rot = [a(f"rot{r}", [P, 2, BLK]) for r in range(2)]
        rot_hi = [a(f"rot_hi{r}", [P, 2, BLK], F32R) for r in range(2)]
        rot_lo = [a(f"rot_lo{r}", [P, 2, BLK], F32R) for r in range(2)]
        assert a.at <= V_AT, a.at

        b = Place(nc, fixed.at)
        q_st, k_st = [], []
        q_st.append(b("q_st0", [P, 2, SEQ], F32R))
        k_st.append(b("k_st0", [P, 2, SEQ], F32R))
        q_st.append(b("q_st1", [P, 2, SEQ], F32R))
        assert b.at == fixed.at + 3 * KT * DIM * 4
        SMALL_AT = b.at
        mask = b("mask", [P, BLK])
        v_pair = [b(f"v_pair{r}", [P, QB, 2, 2 * HD]) for r in range(2)]
        row_max[0] = b("row_max0", [P, 2, 2, QB])
        m_parts = b("m_parts", [P, 2, 2, QB], F32R)
        m_turned = [b(f"m_turned{s}", [P, 32]) for s in range(SLOTS)]
        K1_AT = b.at
        k_st.append(b("k_st1", [P, 2, SEQ], F32R))
        assert b.at <= fixed.at + (3 + 2) * KT * DIM * 4
        gate_sb = b("gate_sb", [P, KT, INNER])
        up_sb = b("up_sb", [P, KT, INNER])
        MASKED_AT = b.at
        masked = [b(f"masked{n}", [P, BLK]) for n in range(MAX_BANKS + 1)]
        assert OWN_AT <= MASKED_AT and b.at <= OWN_END
        for s in range(2, SLOTS):
            q_st.append(b(f"q_st{s}", [P, 2, SEQ], F32R))
            k_st.append(b(f"k_st{s}", [P, 2, SEQ], F32R))
        probs = b("probs", [P, P_RING, 2, BLK])
        assert b.at <= V_AT, b.at

        early = Place(nc, fixed.at)
        wo_hi = early("wo_hi", [P, KT, DIM], F32R)
        wo_raw = Place(nc, early.at)("wo_raw", [P, KT, DIM])
        wo_lo = early("wo_lo", [P, KT, DIM], F32R)
        attn_hi = early("attn_hi", [P, KT, BLK], F32R)
        assert early.at <= SMALL_AT
        h_hi = [early(f"h_hi{r}", [P, BLK], F32R) for r in range(2)]
        hid = early("hid", [P, BLK])
        assert early.at <= K1_AT
        attn = Place(nc, K1_AT)("attn", [P, KT, BLK])
        attn_lo = Place(nc, K1_AT)("attn_lo", [P, KT, BLK], F32R)
        norm_tok = attn
        d = Place(nc, MASKED_AT)
        res = [d(f"res{r}", [P, ST, DIM]) for r in range(2)]
        nx_hi = [d(f"nx_hi{r}", [P, KT, BLK], F32R) for r in range(2)]
        nx_lo = [d(f"nx_lo{r}", [P, KT, BLK], F32R) for r in range(2)]
        g_hi = [d(f"g_hi{r}", [P, KT, P], F32R) for r in range(2)]
        g_lo = [d(f"g_lo{r}", [P, KT, P], F32R) for r in range(2)]
        u_hi = [d(f"u_hi{r}", [P, KT, P], F32R) for r in range(2)]
        u_lo = [d(f"u_lo{r}", [P, KT, P], F32R) for r in range(2)]
        d_hi = [d(f"d_hi{r}", [P, DIM], F32R) for r in range(2)]
        d_lo = [d(f"d_lo{r}", [P, DIM], F32R) for r in range(2)]
        h_lo = [d(f"h_lo{r}", [P, BLK], F32R) for r in range(2)]
        DOWN_AT = TOP - IT * DIM * 4
        down_sb = Place(nc, DOWN_AT)("down_sb", [P, IT, DIM])
        assert d.at <= DOWN_AT, d.at

        psum = ctx.enter_context(nc.psum_tensor("psum", [P, 8, BLK], F32))
        bank = [psum[:, n, :] for n in range(8)]
        proj_ps = [bank[0:2], bank[2:4]]
        v_ps = bank[4:6]
        max_ps = bank[0:3]
        st_ps = [psum[:, 3 + 2 * n:5 + 2 * n, :] for n in range(ST_RING)]
        o_ps = bank[7]
        y_ps = bank[0:4]
        gate_ps, up_ps = bank[4], bank[5]

        def c_ps(n, i):
            return max_ps[i % 2] if n == 0 else bank[6 + i % 2]

        tables_in = sem("tables_in")
        lnw_in = sem("lnw_in")
        first_in = [sem(f"first_in{k}") for k in range(KT)]
        second_in = [sem(f"second_in{k}") for k in range(KT)]
        third_in = sem("third_in")
        x_in = [sem(f"x_in{j}") for j in range(2)]
        w_hi_done = sem("w_hi_done")
        w_lo_done = sem("w_lo_done")
        x_hi_done = sem("x_hi_done")
        x_lo_done = sem("x_lo_done")
        proj_done = sem("proj_done")
        proj_free = sem("proj_free")
        term_done = sem("term_done")
        rot_free = sem("rot_free")
        rot_done = sem("rot_done")
        rot_hi_done = sem("rot_hi_done")
        rot_lo_done = sem("rot_lo_done")
        qk_stored = [sem(f"qk_stored{r}") for r in range(2)]
        v_done = sem("v_done")
        v_free = sem("v_free")
        setup_done = sem("setup_done")
        stack_const = sem("stack_const")
        stack_in = [sem(f"stack_in{s}") for s in range(SLOTS)]
        max_scores = sem("max_scores")
        max_taken = sem("max_taken")
        m_step = sem("m_step")
        m_turned_done = sem("m_turned_done")
        m_in = [sem(f"m_in{s}") for s in range(SLOTS)]
        st_scores = sem("st_scores")
        clamped = sem("clamped")
        exp_done = sem("exp_done")
        v_pair_done = sem("v_pair_done")
        causal_done = sem("causal_done")
        pv_done = sem("pv_done")
        o_copied = sem("o_copied")
        o_stored = [sem(f"o_stored{r}") for r in range(2)]
        dve_waited = sem("dve_waited")
        pool_waited = sem("pool_waited")
        ffn_w_in = sem("ffn_w_in")
        down_in = sem("down_in")
        wo_in = sem("wo_in")
        wo_hi_done = sem("wo_hi_done")
        wo_lo_done = sem("wo_lo_done")
        recip_done = sem("recip_done")
        sums_in = sem("sums_in")
        recip_stored = sem("recip_stored")
        attn_in = [sem(f"attn_in{k}") for k in range(KT)]
        recip_in = [sem(f"recip_in{r}") for r in range(2)]
        res_in = [sem(f"res_in{r}") for r in range(2)]
        attn_scaled = sem("attn_scaled")
        attn_hi_done = sem("attn_hi_done")
        attn_lo_done = sem("attn_lo_done")
        c_done = sem("c_done")
        sum1_done = sem("sum1_done")
        stats_done = sem("stats_done")
        mv1_done = sem("mv1_done")
        pool_step = sem("pool_step")
        rstd1_done = sem("rstd1_done")
        rms_done = sem("rms_done")
        norm1_done = sem("norm1_done")
        norm_tok_done = sem("norm_tok_done")
        turned_done = sem("turned_done")
        nx_hi_done = sem("nx_hi_done")
        nx_lo_done = sem("nx_lo_done")
        gu_hi_done = sem("gu_hi_done")
        gu_lo_done = sem("gu_lo_done")
        gate_done = sem("gate_done")
        up_done = sem("up_done")
        silu_done = sem("silu_done")
        hid_done = sem("hid_done")
        h_hi_done = sem("h_hi_done")
        h_lo_done = sem("h_lo_done")
        d_hi_done = sem("d_hi_done")
        d_lo_done = sem("d_lo_done")
        down_done = sem("down_done")
        sum2_done = sem("sum2_done")
        mv2_done = sem("mv2_done")
        rstd2_done = sem("rstd2_done")
        out_ready = sem("out_ready")
        out_stored = [sem(f"out_stored{r}") for r in range(2)]

        def plain(ap):
            return ap.bitcast(F32)

        def by_tile(dram):
            return dram.rearrange("(k p) n -> p k n", p=P)

        xT_tiles, x_tiles, out_tiles = by_tile(xT), by_tile(x), by_tile(out)
        PAIRS = [(0, 0), (0, 1), (1, 0)]
        FFN_STEPS = IT

        def ffn_done(n, i):
            return n * FFN_STEPS + i + 1

        block = ctx.enter_context(nc.Block())

        @block.sync
        def _(sp):
            for k in range(KT):
                sp.dma_start(w_raw[0][:, k, :], by_tile(wqT)[:, k, :]).then_inc(first_in[k], 16)
                sp.dma_start(x_raw[0][:, k, :], xT_tiles[:, k, 0:BLK]).then_inc(first_in[k], 16)
            for k in range(KT):
                sp.dma_start(w_raw[1][:, k, :], by_tile(wkT)[:, k, :]).then_inc(second_in[k], 16)
            sp.dma_start(cos_sb[:], cos.broadcast_to((P, SEQ))).then_inc(tables_in, 16)
            sp.dma_start(sin_sb[:], sin.broadcast_to((P, SEQ))).then_inc(tables_in, 16)
            sp.dma_start(w_raw[2][:], by_tile(wvT)).then_inc(third_in, 16)
            sp.dma_start(x_raw[1][:], xT_tiles[:, :, BLK:2 * BLK]).then_inc(x_in[1], 16)
            sp.dma_start(lnw_sb[:], ln_w).then_inc(lnw_in, 16)

            def all_stored(blocks):
                for r in range(2):
                    sp.wait_ge(qk_stored[r], 1 + 16 * 4 * 2 * blocks)

            def load(t, j):
                at_least(sp, st_scores, (t - SLOTS + 1) * PAIRS_STEP)
                if isinstance(t, int) and t < SLOTS:
                    sp.wait_ge(stack_const, 2 * (t + 1))
                s = j % SLOTS
                for h in range(2):
                    head = t * 2 + h
                    for part in range(2):
                        src = qk_steps[0, bass.ds(head, 1), part, :, :].broadcast_to((2, HD, SEQ))
                        sp.dma_start(plain(q_st[s][part * 2 * HD:(part + 1) * 2 * HD, h, :]), src)\
                            .then_inc(stack_in[s], 16)
                    src = qk_steps[1, bass.ds(head, 1), :, :, :].rearrange("o a r n -> o (a r) n")
                    sp.dma_start(plain(k_st[s][0:PARTS, h, :]), src.broadcast_to((2, 2 * HD, SEQ)))\
                        .then_inc(stack_in[s], 16)

            def place_maxima(t, j):
                sp.wait_ge(m_turned_done, t + 1)
                rows = plain(q_st[j % SLOTS][MROW:MROW + 2, :, :]).rearrange(
                    "p h (g c x) -> p (h g) c x", c=4, x=32)
                for c in range(4):
                    sp.dma_start(rows[:, :, c, :], m_turned[j % SLOTS][32 * c:32 * c + 32, :])\
                        .then_inc(m_in[j % SLOTS], 16)

            def store_output(t, j):
                r = j % 2
                sp.wait_ge(o_copied, t + 1)
                for c in range(2):
                    sp.dma_start(o_steps[bass.ds(t * 2, 2), :, c * BLK:(c + 1) * BLK],
                                 o_sb[r][c * 64:(c + 1) * 64, :]).then_inc(o_stored[r], 16)

            for tb in range(NBLK):
                if 1 <= tb < NBLK - 1:
                    sp.wait_ge(x_lo_done, KT * tb)
                    sp.dma_start(x_raw[(tb + 1) % 2][:], xT_tiles[:, :, (tb + 1) * BLK:(tb + 2) * BLK])\
                        .then_inc(x_in[(tb + 1) % 2], 16)
                cols = slice(tb * BLK % SEQ, tb * BLK % SEQ + BLK)
                for g in range(4):
                    if tb == NBLK - 1 and g == 1:
                        all_stored(SEQ // BLK)
                        load(0, 0)
                        load(1, 1)
                    sp.wait_ge(rot_lo_done, 4 * tb + g + 1)
                    heads = slice(g % 2 * 16, g % 2 * 16 + 16)
                    for e in range(2):
                        for part, src in enumerate((rot_hi[g % 2], rot_lo[g % 2])):
                            sp.dma_start(qk_dram[g // 2, tb * BLK // SEQ, heads, part,
                                                 e * HALF:(e + 1) * HALF, cols],
                                         plain(src[:, e, :])).then_inc(qk_stored[g % 2], 16)

            all_stored(NBLK)
            for t in range(SLOTS):
                if t >= 3:
                    store_output(t - 3, t - 3)
                load(t + 2, t + 2)
                place_maxima(t, t)
                sp.dma_start(gate_sb[:, t, :], by_tile(gateT)[:, t, :]).then_inc(ffn_w_in, 16)
            with sp.Fori(1, STEPS // SLOTS - 1) as i:
                for j in range(SLOTS):
                    store_output(i * SLOTS + (j - 3), j - 3)
                    if j < 2:
                        load(i * SLOTS + j + 2, j + 2)
                    else:
                        load(i * SLOTS + SLOTS + j - 2, j - 2)
                    place_maxima(i * SLOTS + j, j)

            def load_sums(b_):
                for r in range(2):
                    sp.wait_ge(o_stored[r], 16 * PAIRS_BATCH * (b_ + 1))
                if b_:
                    sp.wait_ge(attn_scaled, KT - 1)
                sp.dma_start(sums, o_dram[b_, :, HD, :].rearrange("h (c n) -> h c n", n=SUMS))\
                    .then_inc(sums_in, 16)

            def spread_recip(b_):
                sp.wait_ge(recip_done, b_ + 1)
                sp.dma_start(r_dram[b_].rearrange("h (c n) -> (h c) n", n=SUMS), sums).then_inc(recip_stored, 16)
                sp.wait_ge(recip_stored, 16 * (b_ + 1))

            def place(n):
                return n * BLK // SEQ, slice(n * BLK % SEQ, n * BLK % SEQ + BLK)

            def load_attn(n):
                if n:
                    sp.wait_ge(turned_done, n * KT)
                b_, cols = place(n)
                for k in range(KT):
                    sp.dma_start(attn[:, k, :], o_dram[b_, 8 * k:8 * k + 8, 0:HD, cols]).then_inc(attn_in[k], 16)

            def load_recip(n, ks):
                b_, cols = place(n)
                for k in ks:
                    at_least(sp, attn_scaled, n * KT + k - 1)
                    src = r_dram[b_, 8 * k:8 * k + 8, cols].rearrange("h (o n) -> h o n", o=1)
                    sp.dma_start(recip[k % 2][:], src.broadcast_to((8, HD, BLK))).then_inc(recip_in[k % 2], 16)

            def load_res(n):
                if n >= 2:
                    sp.wait_ge(out_stored[n % 2], 16 * (n // 2))
                sp.dma_start(res[n % 2][:], x_tiles[:, n * ST:(n + 1) * ST, :]).then_inc(res_in[n % 2], 16)

            def store(n):
                sp.wait_ge(out_ready, ST * (n + 1))
                sp.dma_start(out_tiles[:, n * ST:(n + 1) * ST, :], res[n % 2][:]).then_inc(out_stored[n % 2], 16)

            load_sums(0)
            for t in range(STEPS - SLOTS, STEPS):
                store_output(t - 3, t - 3)
                if t == STEPS - 1:
                    sp.wait_ge(st_scores, (STEPS - 2) * PAIRS_STEP)
                    load_attn(0)
                if t + 2 < STEPS:
                    load(t + 2, t + 2)
                place_maxima(t, t)
                if t + 2 < STEPS:
                    for k in range(2 * (t + SLOTS - STEPS), 2 * (t + SLOTS - STEPS) + 2):
                        sp.dma_start(up_sb[:, k, :], by_tile(upT)[:, k, :]).then_inc(ffn_w_in, 16)
                if t == STEPS - 2:
                    sp.wait_ge(st_scores, (STEPS - 3) * PAIRS_STEP)
                    sp.dma_start(wo_raw[:], by_tile(woT)).then_inc(wo_in, 16)
                    spread_recip(0)
                    load_recip(0, range(2))
            sp.wait_ge(max_taken, STEPS * UNITS)
            load_res(0)
            load_recip(0, range(2, KT))
            store_output(STEPS - 3, STEPS - 3)
            sp.wait_ge(v_pair_done, STEPS)
            sp.dma_start(down_sb[:], by_tile(downT)).then_inc(down_in, 16)
            for t in range(STEPS - 2, STEPS):
                store_output(t, t)
            sp.wait_ge(pv_done, STEPS * QB)
            load_res(1)
            load_sums(1)
            spread_recip(1)
            for n in range(NBLK):
                if n + 1 < NBLK:
                    load_attn(n + 1)
                    load_recip(n + 1, range(2))
                if n >= 1:
                    store(n - 1)
                    if n + 1 < NBLK:
                        load_res(n + 1)
                if n + 1 < NBLK:
                    load_recip(n + 1, range(2, KT))
            n = NBLK - 1
            for s in range(ST):
                sp.wait_ge(out_ready, ST * n + s + 1)
                sp.dma_start(out_tiles[:, n * ST + s, :], res[n % 2][:, s, :]).then_inc(out_stored[n % 2], 16)
            for r in range(2):
                sp.wait_ge(out_stored[r], 16 * (NBLK // 2 + (ST - 1) * r))

        @block.gpsimd
        def _(pool):
            pool.sem_inc(proj_free, 2)
            pool.sem_inc(rot_free, 2)
            pool.sem_inc(v_free, 2)
            pool.sem_inc(qk_stored[0], 1)
            pool.sem_inc(qk_stored[1], 1)
            pool.sem_inc(down_done, 1)
            nc.gpsimd.memset(mhalf, -0.5)
            nc.gpsimd.memset(ident[:], 0.0).then_inc(setup_done, 1)
            pool.wait_ge(setup_done, 1)
            nc.gpsimd.affine_select(out=ident[:], in_=ident[:], compare_op=ALU.not_equal, fill=1.0, base=0,
                                    pattern=[[-1, P]], channel_multiplier=1).then_inc(setup_done, 1)

            def stack_constants(stacks):
                for stack in stacks:
                    nc.gpsimd.memset(plain(stack[PARTS:P, :, :]), 0.0 if stack in q_st else 1.0)\
                        .then_inc(stack_const, 1)

            def rotated_lo(n, j):
                for g in range(4):
                    use = n * 8 + j * 4 + g
                    pool.wait_ge(rot_hi_done, use + 1)
                    nc.gpsimd.tensor_tensor(rot_lo[g % 2][:], rot[g % 2][:], plain(rot_hi[g % 2][:]),
                                            ALU.subtract).then_inc(rot_lo_done, 1)
                    pool.wait_ge(rot_lo_done, use + 1)
                    pool.sem_inc(rot_free, 1)

            with pool.Fori(0, NBLK // 2 - 1) as n:
                for j in range(2):
                    rotated_lo(n, j)
            rotated_lo(NBLK // 2 - 1, 0)

            pool.wait_ge(x_lo_done, KT * NBLK)
            nc.gpsimd.memset(mask[:], 0.0).then_inc(setup_done, 1)
            pool.wait_ge(setup_done, 3)
            nc.gpsimd.affine_select(out=mask[:, BLK - P:BLK], in_=mask[:, BLK - P:BLK], compare_op=ALU.is_ge,
                                    fill=MASKED, base=0, pattern=[[-1, P]], channel_multiplier=1)\
                .then_inc(setup_done, 1)
            pool.wait_ge(setup_done, 4)
            stack_constants([q_st[0], k_st[0], q_st[1], k_st[1]])
            pool.wait_ge(stack_const, 4)
            for r in range(2):
                nc.gpsimd.memset(v_pair[r][:], 1.0).then_inc(setup_done, 1)
            pool.wait_ge(setup_done, 6)
            rotated_lo(NBLK // 2 - 1, 1)
            for r in range(2):
                pool.wait_ge(qk_stored[r], 1 + 16 * 4 * 2 * NBLK)
            pool.wait_ge(v_free, 2 + NBLK * ST)
            stack_constants([q_st[2], k_st[2], q_st[3], k_st[3]])
            pool.wait_ge(stack_const, 2 * SLOTS)

            def step(t, j):
                at_least(pool, pv_done, (t - 1) * QB)
                src = v_sb[:, bass.ds(t, 1), :, :]
                nc.gpsimd.tensor_copy(v_pair[j % 2][:, :, :, 0:HD],
                                      src.rearrange("p o k (h d) -> p (o k) h d", h=2)).then_inc(v_pair_done, 1)
                for kb in range(QB):
                    p = pairs_of(kb)[0]
                    pool.wait_ge(exp_done, t * PAIRS_STEP + p + 1)
                    pool.sem_inc(pool_waited, 1)
                    p2 = probs[:, p % P_RING, :, 0:P]
                    nc.gpsimd.affine_select(out=p2, in_=p2, compare_op=ALU.is_ge, fill=0.0, base=0,
                                            pattern=[[0, 2], [1, P]], channel_multiplier=-1)\
                        .then_inc(causal_done, 1)

            for_steps(pool, step)

            steps = [0]

            def link(ins):
                steps[0] += 1
                ins.then_inc(pool_step, 1)
                pool.wait_ge(pool_step, steps[0])

            def first_norm(n):
                pool.wait_ge(mv1_done, ST * (n + 1))
                if n:
                    pool.wait_ge(norm_tok_done, ST * n)
                mean_var = mv1[:, :, 1]
                link(nc.gpsimd.tensor_scalar(var_eps, mean_var, EPS, None, ALU.add))
                nc.gpsimd.tensor_tensor(rstd1, var_eps, mhalf, ALU.pow).then_inc(rstd1_done, 1)
                pool.wait_ge(rstd1_done, n + 1)
                link(nc.gpsimd.tensor_tensor(ms_eps, rstd1, rstd1, ALU.mult))
                link(nc.gpsimd.tensor_tensor(ms_eps, ms_eps, mean_var, ALU.mult))
                link(nc.gpsimd.tensor_scalar(ms_eps, ms_eps, EPS, None, ALU.add))
                nc.gpsimd.tensor_tensor(rms, ms_eps, mhalf, ALU.pow).then_inc(rms_done, 1)

            def second_norm(n):
                pool.wait_ge(mv2_done, ST * (n + 1))
                if n:
                    pool.wait_ge(out_ready, ST * n)
                link(nc.gpsimd.tensor_scalar(var_eps2, mv2[:, :, 1], EPS, None, ALU.add))
                nc.gpsimd.tensor_tensor(rstd2, var_eps2, mhalf, ALU.pow).then_inc(rstd2_done, 1)

            first_norm(0)
            for n in range(NBLK):
                if n >= 1:
                    second_norm(n - 1)
                if n + 1 < NBLK:
                    first_norm(n + 1)
            n = NBLK - 1
            pool.wait_ge(out_ready, ST * n)
            for s in range(ST):
                pool.wait_ge(mv2_done, ST * n + s + 1)
                tile = slice(s, s + 1)
                link(nc.gpsimd.tensor_scalar(var_eps2[:, tile], mv2[:, tile, 1], EPS, None, ALU.add))
                nc.gpsimd.tensor_tensor(rstd2[:, tile], var_eps2[:, tile], mhalf[:, tile], ALU.pow)\
                    .then_inc(rstd2_done, 1)

        @block.scalar
        def _(act):
            def x_hi_of(tb):
                if tb:
                    act.wait_ge(x_in[tb % 2], (tb + 1) // 2 * 16)
                for k in range(KT):
                    nc.scalar.copy(x_hi[tb % 2][:, k, :], x_raw[tb % 2][:, k, :]).then_inc(x_hi_done, 1)

            for k in range(KT):
                act.wait_ge(first_in[k], 32)
                nc.scalar.copy(w_hi[0][:, k, :], w_raw[0][:, k, :]).then_inc(w_hi_done, 1)
                nc.scalar.copy(x_hi[0][:, k, :], x_raw[0][:, k, :]).then_inc(x_hi_done, 1)
            for k in range(KT):
                act.wait_ge(second_in[k], 16)
                nc.scalar.copy(w_hi[1][:, k, :], w_raw[1][:, k, :]).then_inc(w_hi_done, 1)
            act.wait_ge(third_in, 16)
            nc.scalar.copy(w_hi[2][:], w_raw[2][:]).then_inc(w_hi_done, 1)
            def v_out(tb, s):
                act.wait_ge(v_done, tb * ST + s + 1)
                first, kb = tb * BLK // SEQ * PAIRS_BATCH, (tb * ST + s) % QB
                nc.scalar.copy(v_sb[:, first:first + PAIRS_BATCH, kb, :],
                               v_ps[s % 2].rearrange("p (t n) -> p t n", n=2 * HD)).then_inc(v_free, 1)

            for tb in range(NBLK):
                for g in range(4):
                    if g == 3:
                        v_out(tb, 0)
                    act.wait_ge(rot_done, tb * 4 + g + 1)
                    act.wait_ge(qk_stored[g % 2], tb * 128 + g // 2 * 64 + 1)
                    nc.scalar.copy(rot_hi[g % 2][:], rot[g % 2][:]).then_inc(rot_hi_done, 1)
                    if g == 0 and tb + 1 < NBLK:
                        x_hi_of(tb + 1)
                for s in range(1, ST):
                    v_out(tb, s)

            def exps(t, first, last):
                for p in range(first, last):
                    kb, c, q0, w = ST_PAIRS[p]
                    scores, to = st_ps[p % ST_RING], probs[:, p % P_RING]
                    act.wait_ge(st_scores, t * PAIRS_STEP + p + 1)
                    skip = P if w == P else 0
                    diagonal = q0 == kb * P
                    if diagonal:
                        square = scores[:, :, skip:skip + P]
                        nc.scalar.activation(square, square, ACT.Relu, scale=-1.0).then_inc(clamped, 1)
                    before = ST_PAIRS[(p - P_RING) % PAIRS_STEP][0]
                    at_least(act, pv_done, (t if p >= P_RING else t - 1) * QB + before + 1)
                    if diagonal:
                        if w > P:
                            nc.scalar.activation(to[:, :, P:w], scores[:, :, P:w], ACT.Exp, scale=SCALE)
                        act.wait_ge(clamped, t * QB + kb + 1)
                        nc.scalar.activation(to[:, :, 0:P], square, ACT.Exp, scale=-SCALE).then_inc(exp_done, 1)
                    else:
                        nc.scalar.activation(to, scores, ACT.Exp, scale=SCALE).then_inc(exp_done, 1)

            def output(t, j):
                act.wait_ge(pv_done, t * QB)
                r = (j - 1) % 2
                if isinstance(t, int):
                    at_least(act, o_stored[r], (t - 1) // 2 * 32)
                else:
                    act.wait_ge(o_stored[r], (t - j) * 16 + (j - 1) // 2 * 32)
                nc.scalar.copy(o_sb[r][:], o_ps).then_inc(o_copied, 1)

            def step(t, j):
                exps(t, 0, PV_LAG)
                if not (isinstance(t, int) and t == 0):
                    output(t, j)
                exps(t, PV_LAG, PAIRS_STEP)

            for_steps(act, step)
            output(STEPS, STEPS)

            def attn_part(n, k):
                act.wait_ge(attn_scaled, n * KT + k + 1)
                if isinstance(k, int):
                    src, to = attn[:, k, :], attn_hi[:, k, :]
                else:
                    src, to = attn[:, bass.ds(k, 1), :], attn_hi[:, bass.ds(k, 1), :]
                nc.scalar.copy(to, src).then_inc(attn_hi_done, 1)

            def turned_parts(n, ks):
                at_least(act, up_done, (n - 1) * FFN_STEPS)
                for k in ks:
                    act.wait_ge(turned_done, n * KT + k + 1)
                    nc.scalar.activation(nx_hi[n % 2][:, k, :], c_ps(n, k), ACT.Copy,
                                         scale=lnw_sb[:, k:k + 1]).then_inc(nx_hi_done, 1)

            def gate_up_hi(n, i, r):
                at_least(act, up_done, n * FFN_STEPS + i - 1)
                cols = slice(i * P, (i + 1) * P) if isinstance(i, int) else bass.ds(i * P, P)
                nc.scalar.copy(g_hi[r][:], gate_sb[:, :, cols]).then_inc(gu_hi_done, 1)
                nc.scalar.copy(u_hi[r][:], up_sb[:, :, cols]).then_inc(gu_hi_done, 1)

            def silu_of(n, i, r):
                act.wait_ge(gate_done, n * FFN_STEPS + i + 1)
                at_least(act, h_lo_done, n * FFN_STEPS + i)
                nc.scalar.activation(hid[:], gate_ps, ACT.Silu).then_inc(silu_done, 1)
                at_least(act, down_done, n * FFN_STEPS + i)
                src = down_sb[:, i, :] if isinstance(i, int) else \
                    down_sb[:, bass.ds(i, 1), :].rearrange("p o n -> p (o n)")
                nc.scalar.copy(d_hi[r][:], src).then_inc(d_hi_done, 1)

            def ffn_step(n, i, r):
                gate_up_hi(n, i, r)
                silu_of(n, i - 1, 1 - r)

            def ffn_steps(n, first, last):
                with act.Fori(first // 2, last // 2) as i:
                    for r in range(2):
                        ffn_step(n, i * 2 + r, r)

            act.wait_ge(lnw_in, 16)
            act.wait_ge(ffn_w_in, 32 * KT)
            gate_up_hi(0, 0, 0)
            turned_parts(0, range(KT))
            act.wait_ge(down_in, 16)
            for n in range(NBLK):
                if n >= 1:
                    gate_up_hi(n, 0, 0)
                    silu_of(n - 1, IT - 1, 1)
                ffn_step(n, 1, 1)
                ffn_steps(n, 2, 4)
                if n + 1 == NBLK:
                    ffn_steps(n, 4, IT)
                    continue
                with act.Fori(2, 4) as i:
                    for r in range(2):
                        ffn_step(n, i * 2 + r, r)
                        if r == 0:
                            act.wait_ge(c_done, (n + 1) * ST)
                        attn_part(n + 1, i * 2 + (r - 4))
                ffn_steps(n, 8, 10)
                ffn_steps(n, 10, 12)
                for r in range(2):
                    turned_parts(n + 1, (2 * r, 2 * r + 1))
                    ffn_step(n, 12 + r, r)
            silu_of(NBLK - 1, IT - 1, 1)

        @block.vector
        def _(dve):
            def x_lo_of(tb, ks):
                for k in ks:
                    dve.wait_ge(x_hi_done, tb * KT + k + 1)
                    nc.vector.tensor_tensor(x_lo[tb % 2][:, k, :], x_raw[tb % 2][:, k, :],
                                            plain(x_hi[tb % 2][:, k, :]), ALU.subtract).then_inc(x_lo_done, 1)

            for k in range(KT):
                dve.wait_ge(w_hi_done, k + 1)
                nc.vector.tensor_tensor(w_lo[0][:, k, :], w_raw[0][:, k, :], plain(w_hi[0][:, k, :]),
                                        ALU.subtract).then_inc(w_lo_done, 1)
                x_lo_of(0, (k,))
            for k in range(KT):
                dve.wait_ge(w_hi_done, KT + k + 1)
                nc.vector.tensor_tensor(w_lo[1][:, k, :], w_raw[1][:, k, :], plain(w_hi[1][:, k, :]),
                                        ALU.subtract).then_inc(w_lo_done, 1)
            dve.wait_ge(tables_in, 32)
            for tb in range(NBLK):
                cos_j, sin_j = (t[:, tb % 2 * BLK:(tb % 2 + 1) * BLK] for t in (cos_sb, sin_sb))
                for g in range(4):
                    use = tb * 4 + g
                    even, odd = proj_ps[g % 2]
                    dve.wait_ge(proj_done, use + 1)
                    nc.vector.tensor_tensor(term[0][:], even, cos_j, ALU.mult)
                    nc.vector.tensor_tensor(term[1][:], odd, sin_j, ALU.mult)
                    nc.vector.tensor_tensor(term[2][:], even, sin_j, ALU.mult)
                    nc.vector.tensor_tensor(term[3][:], odd, cos_j, ALU.mult).then_inc(term_done, 1)
                    dve.wait_ge(term_done, use + 1)
                    dve.sem_inc(proj_free, 1)
                    dve.wait_ge(rot_free, use + 1)
                    nc.vector.tensor_tensor(rot[g % 2][:, 0, :], term[0][:], term[1][:], ALU.subtract)
                    nc.vector.tensor_tensor(rot[g % 2][:, 1, :], term[2][:], term[3][:], ALU.add)\
                        .then_inc(rot_done, 1)
                    dve.wait_ge(rot_done, use + 1)
                    if g == 1 and tb == 0:
                        dve.wait_ge(w_hi_done, 2 * KT + 1)
                        nc.vector.tensor_tensor(w_lo[2][:], w_raw[2][:], plain(w_hi[2][:]), ALU.subtract)\
                            .then_inc(w_lo_done, 1)
                    if 1 <= g < 3 and tb + 1 < NBLK:
                        x_lo_of(tb + 1, (2 * g - 2, 2 * g - 1))

            def negated(t, j, part):
                own = row_max[j % 2]
                if part == 0:
                    dve.wait_ge(max_taken, (t + 1) * UNITS)
                    late = own[:, 0, :, QB // 2:QB]
                    nc.vector.tensor_tensor(late, late, own[:, 1, :, QB // 2:QB], ALU.max).then_inc(m_step, 1)
                elif part == 1:
                    dve.wait_ge(m_step, t * 3 + 1)
                    at_least(dve, m_turned_done, t)
                    nc.vector.tensor_scalar(m_parts[:, 0], own[:, 0], -1.0, None, ALU.mult).then_inc(m_step, 1)
                elif part == 2:
                    dve.wait_ge(m_step, t * 3 + 2)
                    nc.vector.scalar_tensor_tensor(m_parts[:, 1], own[:, 0], -1.0, plain(m_parts[:, 0]),
                                                   ALU.mult, ALU.subtract).then_inc(m_step, 1)
                else:
                    dve.wait_ge(m_step, t * 3 + 3)
                    if isinstance(t, int):
                        at_least(dve, m_in[j % SLOTS], t // SLOTS * 64)
                    else:
                        dve.wait_ge(m_in[j], (t - j) * 16)
                    nc.vector.transpose(m_turned[j % SLOTS][:],
                                        plain(m_parts[:].rearrange("p a h q -> p (a h q)")))\
                        .then_inc(m_turned_done, 1)

            dve.wait_ge(setup_done, 4)

            def step(t, j):
                for u, (qb, h, c, w) in enumerate(MAX_UNITS):
                    diagonal = c + w == (qb + 1) * P
                    dve.wait_ge(max_scores, t * UNITS + u + 1)
                    if diagonal:
                        dve.sem_inc(dve_waited, 1)
                    scores = max_ps[u % MAX_BANKS][:, 0:w]
                    to = row_max[j % 2][:, c // BLK, h, qb:qb + 1]
                    if diagonal:
                        nc.vector.tensor_tensor_reduce(masked[u % (MAX_BANKS + 1)][:, 0:w], scores,
                                                       mask[:, BLK - w:BLK], 1.0, LEAST,
                                                       ALU.add, ALU.max, to).then_inc(max_taken, 1)
                    else:
                        nc.vector.tensor_reduce(to, scores, AX.X, ALU.max).then_inc(max_taken, 1)
                    if u in (1, 3, 5, 7) and not (isinstance(t, int) and t == 0):
                        negated(t - 1, (j - 1) % SLOTS, u // 2)
            def sum_recips(b_):
                dve.wait_ge(sums_in, 16 * (b_ + 1))
                nc.vector.reciprocal(sums, sums).then_inc(recip_done, 1)

            for t in range(SLOTS):
                step(t, t)
            with dve.Fori(1, STEPS // SLOTS - 1) as i:
                for j in range(SLOTS):
                    step(i * SLOTS + j, j)
            for t in range(STEPS - SLOTS, STEPS):
                if t == STEPS - 2:
                    sum_recips(0)
                step(t, t)
            for part in range(4):
                negated(STEPS - 1, STEPS - 1, part)

            def attn_scale(n, k, r):
                use = n * KT + k
                if isinstance(k, int):
                    dve.wait_ge(attn_in[k], 16 * (n + 1))
                    dve.wait_ge(recip_in[r], 16 * (use // 2 + 1))
                    to = attn[:, k, :]
                else:
                    dve.wait_ge(recip_in[r], k * 8 + (n * KT * 8 - r * 8 + 16))
                    to = attn[:, bass.ds(k, 1), :].rearrange("p o n -> p (o n)")
                nc.vector.tensor_tensor(to, to, recip[r][:], ALU.mult).then_inc(attn_scaled, 1)

            def attn_part(n, k):
                dve.wait_ge(attn_hi_done, n * KT + k + 1)
                if isinstance(k, int):
                    lo, src, hi = attn_lo[:, k, :], attn[:, k, :], plain(attn_hi[:, k, :])
                else:
                    at = bass.ds(k, 1)
                    lo, src, hi = attn_lo[:, at, :], attn[:, at, :], plain(attn_hi[:, at, :])
                nc.vector.tensor_tensor(lo, src, hi, ALU.subtract).then_inc(attn_lo_done, 1)

            def tile_stats(src, parts, to, done):
                nc.vector.bn_stats(parts, src).then_inc(stats_done, 1)
                seen[0] += 1
                dve.wait_ge(stats_done, seen[0])
                nc.vector.bn_aggr(to, parts).then_inc(done, 1)

            seen = [0]

            def first_sum(n):
                dve.wait_ge(res_in[n % 2], 16 * (n // 2 + 1))
                if n:
                    dve.wait_ge(rms_done, n)
                    dve.wait_ge(norm1_done, ST * n)
                for s in range(ST):
                    z = res[n % 2][:, s, :]
                    dve.wait_ge(c_done, n * ST + s + 1)
                    nc.vector.tensor_tensor(z, c_ps(n, s), z, ALU.add).then_inc(sum1_done, 1)
                    dve.wait_ge(sum1_done, n * ST + s + 1)
                    tile_stats(z, stats[:, 0, s, :], mv1[:, s, :], mv1_done)

            def first_norm(n):
                dve.wait_ge(rstd1_done, n + 1)
                for s in range(ST):
                    z = res[n % 2][:, s, :]
                    nc.vector.tensor_scalar(z, z, mv1[:, s, 0:1], rstd1[:, s:s + 1], ALU.subtract, ALU.mult)\
                        .then_inc(norm1_done, 1)
                dve.wait_ge(rms_done, n + 1)
                for s in range(ST):
                    dve.wait_ge(norm1_done, n * ST + s + 1)
                    nc.vector.tensor_scalar(norm_tok[:, s, :], res[n % 2][:, s, :], rms[:, s:s + 1], None,
                                            ALU.mult).then_inc(norm_tok_done, 1)

            def turned_parts(n, ks):
                for k in ks:
                    dve.wait_ge(nx_hi_done, n * KT + k + 1)
                    nc.vector.scalar_tensor_tensor(nx_lo[n % 2][:, k, :], c_ps(n, k), lnw_sb[:, k:k + 1],
                                                   plain(nx_hi[n % 2][:, k, :]), ALU.mult, ALU.subtract)\
                        .then_inc(nx_lo_done, 1)

            def gate_up_lo(n, i, r):
                done = (n * FFN_STEPS + i) * 2
                cols = slice(i * P, (i + 1) * P) if isinstance(i, int) else bass.ds(i * P, P)
                dve.wait_ge(gu_hi_done, done + 1)
                nc.vector.tensor_tensor(g_lo[r][:], gate_sb[:, :, cols], plain(g_hi[r][:]), ALU.subtract)\
                    .then_inc(gu_lo_done, 1)
                dve.wait_ge(gu_hi_done, done + 2)
                nc.vector.tensor_tensor(u_lo[r][:], up_sb[:, :, cols], plain(u_hi[r][:]), ALU.subtract)\
                    .then_inc(gu_lo_done, 1)

            def hidden(n, i, r):
                done = n * FFN_STEPS + i
                dve.wait_ge(silu_done, done + 1)
                dve.wait_ge(up_done, done + 1)
                nc.vector.tensor_tensor(hid[:], up_ps, hid[:], ALU.mult).then_inc(hid_done, 1)
                dve.wait_ge(hid_done, done + 1)
                at_least(dve, down_done, done)
                nc.vector.tensor_copy(h_hi[r][:], hid[:]).then_inc(h_hi_done, 1)
                dve.wait_ge(h_hi_done, done + 1)
                nc.vector.tensor_tensor(h_lo[r][:], hid[:], plain(h_hi[r][:]), ALU.subtract)\
                    .then_inc(h_lo_done, 1)
                dve.wait_ge(d_hi_done, done + 1)
                src = down_sb[:, i, :] if isinstance(i, int) else \
                    down_sb[:, bass.ds(i, 1), :].rearrange("p o n -> p (o n)")
                nc.vector.tensor_tensor(d_lo[r][:], src, plain(d_hi[r][:]), ALU.subtract).then_inc(d_lo_done, 1)

            def second_sum(n):
                dve.wait_ge(down_done, 1 + ffn_done(n, IT - 1))
                for s in range(ST):
                    z = res[n % 2][:, s, :]
                    nc.vector.tensor_tensor(z, y_ps[s], z, ALU.add).then_inc(sum2_done, 1)

            def second_stats(n):
                if n:
                    dve.wait_ge(rstd2_done, n)
                    dve.wait_ge(out_ready, ST * n)
                for s in range(ST):
                    dve.wait_ge(sum2_done, n * ST + s + 1)
                    tile_stats(res[n % 2][:, s, :], stats[:, 1, s, :], mv2[:, s, :], mv2_done)

            def second_norm(n):
                dve.wait_ge(rstd2_done, n + 1)
                for s in range(ST):
                    z = res[n % 2][:, s, :]
                    nc.vector.tensor_scalar(z, z, mv2[:, s, 0:1], rstd2[:, s:s + 1], ALU.subtract, ALU.mult)\
                        .then_inc(out_ready, 1)

            def ffn_step(n, i, r):
                gate_up_lo(n, i, r)
                hidden(n, i - 1, 1 - r)

            def ffn_steps(n, first, last):
                with dve.Fori(first // 2, last // 2) as i:
                    for r in range(2):
                        ffn_step(n, i * 2 + r, r)

            dve.wait_ge(wo_in, 16)
            nc.vector.tensor_copy(wo_hi[:], wo_raw[:]).then_inc(wo_hi_done, 1)
            dve.wait_ge(wo_hi_done, 1)
            nc.vector.tensor_tensor(wo_lo[:], wo_raw[:], plain(wo_hi[:]), ALU.subtract).then_inc(wo_lo_done, 1)
            for k in range(KT):
                attn_scale(0, k, k % 2)
                dve.wait_ge(attn_scaled, k + 1)
                nc.vector.tensor_copy(attn_hi[:, k, :], attn[:, k, :]).then_inc(attn_hi_done, 1)
                attn_part(0, k)
            first_sum(0)
            first_norm(0)
            dve.wait_ge(lnw_in, 16)
            dve.wait_ge(ffn_w_in, 32 * KT)
            gate_up_lo(0, 0, 0)
            turned_parts(0, range(KT))
            dve.wait_ge(down_in, 16)
            for n in range(NBLK):
                if n >= 1:
                    gate_up_lo(n, 0, 0)
                    hidden(n - 1, IT - 1, 1)
                gate_up_lo(n, 1, 1)
                if n >= 1:
                    second_sum(n - 1)
                hidden(n, 0, 0)
                if n >= 1:
                    second_stats(n - 1)
                if n == 0:
                    sum_recips(1)
                ffn_steps(n, 2, 4)
                if n >= 1:
                    second_norm(n - 1)
                if n + 1 == NBLK:
                    ffn_steps(n, 4, IT)
                    continue
                for k in range(KT):
                    dve.wait_ge(attn_in[k], 16 * (n + 2))
                with dve.Fori(2, 4) as i:
                    for r in range(2):
                        ffn_step(n, i * 2 + r, r)
                        k = i * 2 + (r - 4)
                        attn_scale(n + 1, k, r)
                        attn_part(n + 1, k)
                ffn_step(n, 8, 0)
                first_sum(n + 1)
                ffn_step(n, 9, 1)
                first_norm(n + 1)
                ffn_steps(n, 10, 12)
                for r in range(2):
                    turned_parts(n + 1, (2 * r, 2 * r + 1))
                    ffn_step(n, 12 + r, r)
            hidden(NBLK - 1, IT - 1, 1)
            n = NBLK - 1
            dve.wait_ge(rstd2_done, n)
            dve.wait_ge(out_ready, ST * n)

            def last_norm(s):
                dve.wait_ge(rstd2_done, n + s + 1)
                z = res[n % 2][:, s, :]
                nc.vector.tensor_scalar(z, z, mv2[:, s, 0:1], rstd2[:, s:s + 1], ALU.subtract, ALU.mult)\
                    .then_inc(out_ready, 1)

            for s in range(ST):
                z = res[n % 2][:, s, :]
                dve.wait_ge(down_done, 1 + ffn_done(n, IT - 1) + s)
                nc.vector.tensor_tensor(z, y_ps[s], z, ALU.add).then_inc(sum2_done, 1)
                dve.wait_ge(sum2_done, n * ST + s + 1)
                tile_stats(z, stats[:, 1, s, :], mv2[:, s, :], mv2_done)
                if s:
                    last_norm(s - 1)
            last_norm(ST - 1)

        @block.tensor
        def _(pe):
            def product(to, left, right, first=True, last=True):
                for n, (a_, b_) in enumerate(PAIRS):
                    mm = nc.tensor.matmul(to, left[a_], right[b_], start=first and n == 0,
                                          stop=last and n == len(PAIRS) - 1)
                return mm

            def project_qk(n, j):
                for g in range(4):
                    use = n * 8 + j * 4 + g
                    w = g // 2
                    pe.wait_ge(proj_free, use + 1)
                    for half in range(2):
                        cols = slice((g % 2 * 2 + half) * P, (g % 2 * 2 + half + 1) * P)
                        for k in range(KT):
                            if g % 2 == 0 and half == 0:
                                pe.wait_ge(w_lo_done, w * KT + k + 1)
                            if g == 0 and half == 0:
                                pe.wait_ge(x_lo_done, n * 8 + j * 4 + k + 1)
                            mm = product(proj_ps[g % 2][half], (w_hi[w][:, k, cols], w_lo[w][:, k, cols]),
                                         (x_hi[j][:, k, :], x_lo[j][:, k, :]), k == 0, k == KT - 1)
                    mm.then_inc(proj_done, 1)

            def project_v(n, j, s, ks=range(KT)):
                pe.wait_ge(w_lo_done, 2 * KT + 1)
                pe.wait_ge(v_free, n * 8 + j * 4 + s + 1)
                rows = slice(s * P, (s + 1) * P)
                for k in ks:
                    mm = product(v_ps[s % 2], (x_hi[j][:, k, rows], x_lo[j][:, k, rows]),
                                 (w_hi[2][:, k, :], w_lo[2][:, k, :]), k == 0, k == KT - 1)
                if KT - 1 in ks:
                    mm.then_inc(v_done, 1)

            LAST = NBLK // 2 - 1
            with pe.Fori(0, LAST) as n:
                for j in range(2):
                    project_qk(n, j)
                    for s in range(ST):
                        project_v(n, j, s)
            project_qk(LAST, 0)
            for s in range(ST):
                project_v(LAST, 0, s)
            project_qk(LAST, 1)

            def max_scores_of(t, j, units):
                s = j % SLOTS
                for u in units:
                    qb, h, c, w = MAX_UNITS[u]
                    at_least(pe, max_taken, t * UNITS + u + 1 - MAX_BANKS)
                    wide = max(w, 2 * P)
                    nc.tensor.matmul(max_ps[u % MAX_BANKS][:, 0:wide],
                                     q_st[s][0:MROW, h, qb * P:(qb + 1) * P],
                                     k_st[s][0:MROW, h, c:c + wide], start=True, stop=True)\
                        .then_inc(max_scores, 1)

            def st_scores_of(t, j, p):
                s = j % SLOTS
                kb, c, q0, w = ST_PAIRS[p]
                at_least(pe, exp_done, t * PAIRS_STEP + p + 1 - ST_RING)
                wide = max(w, 2 * P)
                q0 -= wide - w
                for h in range(2):
                    mm = nc.tensor.matmul(st_ps[p % ST_RING][:, h, 0:wide],
                                          k_st[s][:, h, kb * P:(kb + 1) * P],
                                          q_st[s][:, h, q0:q0 + wide], start=True, stop=True)
                mm.then_inc(st_scores, 1)

            def values(t, j, kb):
                pe.wait_ge(exp_done, t * PAIRS_STEP + pairs_of(kb)[-1] + 1)
                pe.wait_ge(causal_done, t * QB + kb + 1)
                if kb == 0:
                    pe.wait_ge(v_pair_done, t + 1)
                    at_least(pe, o_copied, t)
                for p in pairs_of(kb):
                    _, c, q0, w = ST_PAIRS[p]
                    for h in range(2):
                        rows = (c * 2 + h) * 32
                        mm = nc.tensor.matmul(o_ps[rows:rows + 2 * HD, q0 - c * BLK:q0 - c * BLK + w],
                                              v_pair[j % 2][:, kb, h, :], probs[:, p % P_RING, h, 0:w],
                                              start=kb == 0, stop=kb == (c + 1) * BLK // P - 1)
                mm.then_inc(pv_done, 1)

            def step(t, j, maxima=True, late=True, between=None):
                fixed_t = isinstance(t, int)
                if maxima:
                    s = j % SLOTS
                    pe.wait_ge(stack_in[s], t // SLOTS * 96 + 96 if fixed_t else (t - j) * 24 + 96)
                s2 = (j - 2) % SLOTS
                if late:
                    uses = (t - 2) // SLOTS * 64 + 64 if fixed_t else (t - j) * 16 + (j - 2) // SLOTS * 64 + 64
                    pe.wait_ge(m_in[s2], uses)
                for p in range(PAIRS_STEP):
                    if maxima:
                        max_scores_of(t, j, (2 * p,))
                    if late:
                        st_scores_of(t - 2, s2, p)
                    if maxima:
                        max_scores_of(t, j, (2 * p + 1,))
                    behind = (p - PV_LAG) % PAIRS_STEP
                    kb = ST_PAIRS[behind][0]
                    if pairs_of(kb)[-1] == behind:
                        if p >= PV_LAG and late:
                            values(t - 2, s2, kb)
                        elif p < PV_LAG and (not fixed_t or t >= 3):
                            values(t - 3, (j - 3) % SLOTS, kb)
                    if between:
                        between(p)

            def rest_of_v(p):
                if V_FROM <= p < V_FROM + 2 * KT:
                    project_v(LAST, 1, 2 + (p - V_FROM) // KT, ((p - V_FROM) % KT,))

            V_FROM = 1
            for s in range(2):
                project_v(LAST, 1, s)
            pe.wait_ge(rot_done, 4 * NBLK)
            step(0, 0, late=False, between=rest_of_v)
            step(1, 1, late=False)
            pe.wait_ge(v_free, 2 + NBLK * ST)
            for t in range(2, SLOTS):
                step(t, t)
            with pe.Fori(1, STEPS // SLOTS) as i:
                for j in range(SLOTS):
                    step(i * SLOTS + j, j)
            def project(n, s, ks=range(KT)):
                rows = slice(s * P, (s + 1) * P)
                at_least(pe, sum1_done, n * ST + s - 1)
                for k in ks:
                    if s == 0:
                        pe.wait_ge(attn_lo_done, n * KT + k + 1)
                    mm = product(c_ps(n, s), (attn_hi[:, k, rows], attn_lo[:, k, rows]),
                                 (wo_hi[:, k, :], wo_lo[:, k, :]), k == 0, k == KT - 1)
                if KT - 1 in ks:
                    mm.then_inc(c_done, 1)

            step(STEPS, STEPS, maxima=False)
            pe.wait_ge(max_taken, STEPS * UNITS)
            pe.wait_ge(wo_lo_done, 1)
            def first_projection(p):
                if C_FROM <= p < C_FROM + 2 * ST:
                    part = (p - C_FROM) % 2
                    project(0, (p - C_FROM) // 2, (2 * part, 2 * part + 1))

            C_FROM = 2
            step(STEPS + 1, STEPS + 1, maxima=False, between=first_projection)
            for kb in range(QB - PV_LAG, QB):
                values(STEPS - 1, (STEPS - 1) % SLOTS, kb)

            pe.wait_ge(o_copied, STEPS)

            def turn(n, ks):
                for k in ks:
                    at_least(pe, nx_lo_done, n * KT + k - 1 if k >= 2 else 0)
                    for s in range(ST):
                        if k == 0:
                            pe.wait_ge(norm_tok_done, n * ST + s + 1)
                        mm = nc.tensor.transpose(c_ps(n, k)[:, s * P:(s + 1) * P],
                                                 norm_tok[:, s, k * P:(k + 1) * P], ident[:])
                    mm.then_inc(turned_done, 1)

            def gate_up(n, i, r):
                done = n * FFN_STEPS + i
                for which, (hi, lo, to, ready, used) in enumerate((
                        (g_hi[r], g_lo[r], gate_ps, gate_done, silu_done),
                        (u_hi[r], u_lo[r], up_ps, up_done, hid_done))):
                    pe.wait_ge(gu_lo_done, done * 2 + which + 1)
                    at_least(pe, used, done)
                    for k in range(KT):
                        if isinstance(i, int) and i == 0 and which == 0:
                            pe.wait_ge(nx_lo_done, n * KT + k + 1)
                        mm = product(to, (hi[:, k, :], lo[:, k, :]),
                                     (nx_hi[n % 2][:, k, :], nx_lo[n % 2][:, k, :]), k == 0, k == KT - 1)
                    mm.then_inc(ready, 1)

            def down(n, i, r, first=False, last=False):
                done = n * FFN_STEPS + i
                pe.wait_ge(h_lo_done, done + 1)
                pe.wait_ge(d_lo_done, done + 1)
                if first:
                    at_least(pe, sum2_done, n * ST)
                for s in range(ST):
                    rows = slice(s * P, (s + 1) * P)
                    mm = product(y_ps[s], (h_hi[r][:, rows], h_lo[r][:, rows]), (d_hi[r][:], d_lo[r][:]),
                                 first, last)
                    if n == NBLK - 1 and last:
                        mm.then_inc(down_done, 1)
                if not (n == NBLK - 1 and last):
                    mm.then_inc(down_done, 1)

            def ffn_step(n, i, r):
                gate_up(n, i, r)
                down(n, i - 1, 1 - r)

            def ffn_steps(n, first, last):
                with pe.Fori(first // 2, last // 2) as i:
                    for r in range(2):
                        ffn_step(n, i * 2 + r, r)

            pe.wait_ge(setup_done, 2)
            turn(0, range(KT))
            gate_up(0, 0, 0)
            for n in range(NBLK):
                if n >= 1:
                    gate_up(n, 0, 0)
                    down(n - 1, IT - 1, 1, last=True)
                gate_up(n, 1, 1)
                down(n, 0, 0, first=True)
                if n + 1 == NBLK:
                    ffn_steps(n, 2, IT)
                    continue
                ffn_steps(n, 2, 8)
                for s in range(ST):
                    project(n + 1, s)
                ffn_steps(n, 8, 10)
                for r in range(2):
                    ffn_step(n, 10 + r, r)
                    turn(n + 1, (2 * r, 2 * r + 1))
                ffn_steps(n, 12, IT)
            down(NBLK - 1, IT - 1, 1, last=True)


def kernel(L0_attn_x, L0_attn_wq, L0_attn_wk, L0_attn_wv, L0_attn_wo, L0_ffn_ln_w, L0_ffn_gate_w,
           L0_ffn_up_w, L0_ffn_down_w):
    import numpy as np
    import concourse.bacc as bacc
    from concourse.bass_utils import run_bass_kernel_spmd

    def turned(w):
        return np.ascontiguousarray(np.asarray(w).T)

    def rotary_rows(w):
        w = np.asarray(w).reshape(2, HEADS // 2, HALF, 2, DIM)
        return turned(w.transpose(0, 3, 1, 2, 4).reshape(DIM, DIM))

    position = np.arange(SEQ, dtype=np.float64)
    x = np.ascontiguousarray(np.asarray(L0_attn_x).reshape(TOK, DIM))
    arrays = {
        "x": x,
        "xT": turned(x),
        "wqT": rotary_rows(L0_attn_wq),
        "wkT": rotary_rows(L0_attn_wk),
        "wvT": turned(L0_attn_wv),
        "woT": turned(L0_attn_wo),
        "ln_w": turned(np.asarray(L0_ffn_ln_w).reshape(KT, P)),
        "gateT": turned(L0_ffn_gate_w),
        "upT": turned(L0_ffn_up_w),
        "downT": turned(L0_ffn_down_w),
        "cos": np.cos(position).astype(np.float32).reshape(1, SEQ),
        "sin": np.sin(position).astype(np.float32).reshape(1, SEQ),
    }
    nc = bacc.Bacc("TRN2", target_bir_lowering=False, num_devices=1)
    args = {name: nc.dram_tensor(name, a.shape, mybir.dt.from_np(a.dtype), kind="ExternalInput").ap()
            for name, a in arrays.items()}
    out = nc.dram_tensor("out", (TOK, DIM), F32, kind="ExternalOutput").ap()
    layer_kernel(nc, **args, out=out)
    result = run_bass_kernel_spmd(nc, [arrays], core_ids=[0])
    return result.results[0]["out"].reshape(BATCH, SEQ, DIM)
```
